# Optimizing a Trainium2 kernel written in Bass

```python
import numpy as np
import jax
import jax.numpy as jnp

def _softmax(x, axis=-1):
    return jax.nn.softmax(x, axis=axis)

def _gelu(x):
    return jax.nn.gelu(x, approximate=True)

def _silu(x):
    return jax.nn.silu(x)

def _sigmoid(x):
    return jax.nn.sigmoid(x)

def _layernorm(x, axis=-1, eps=1e-05):
    m = jnp.mean(x, axis=axis, keepdims=True)
    v = jnp.var(x, axis=axis, keepdims=True)
    return (x - m) / jnp.sqrt(v + eps)

def _scatter_add(tgt, idx, src, axis=0):
    return tgt.at[idx].add(src)

def _segment_sum(src, seg, n):
    return jax.ops.segment_sum(src, seg, n)
kernel_name = 'mk_dlrm_tower_d1_rec_r8_d4822a'

def setup_inputs(seed: int=0):
    np.random.seed(seed)
    _w = jnp.asarray

    def _rec_inputs():
        import jax
        import jax.numpy as jnp
        _tk = jax.random.key(seed)
        dense_ctx = jax.random.normal(jax.random.fold_in(_tk, 190), (512, 16), jnp.float32)
        ids = jnp.stack([jax.random.randint(jax.random.fold_in(_tk, 200 + f), (512,), 0, v, jnp.int32) for f, v in enumerate([12500, 12500, 12500, 1250, 1000, 12500, 12500, 125000, 1250, 1250, 1250, 125000, 12500, 12500, 12500, 125000, 1250, 125000, 1000, 125000, 1000, 1250, 12500, 1250, 1250, 125000, 1250, 12500, 1000, 12500, 1250, 1000, 12500, 12500, 1250, 12500, 1000, 1250, 12500])], axis=1)
        tbl_0 = 0.05 * jax.random.normal(jax.random.fold_in(_tk, 500 + 0), (12500, 32), jnp.float32)
        tbl_1 = 0.05 * jax.random.normal(jax.random.fold_in(_tk, 500 + 1), (12500, 32), jnp.float32)
        tbl_2 = 0.05 * jax.random.normal(jax.random.fold_in(_tk, 500 + 2), (12500, 32), jnp.float32)
        tbl_3 = 0.05 * jax.random.normal(jax.random.fold_in(_tk, 500 + 3), (1250, 32), jnp.float32)
        tbl_4 = 0.05 * jax.random.normal(jax.random.fold_in(_tk, 500 + 4), (1000, 32), jnp.float32)
        tbl_5 = 0.05 * jax.random.normal(jax.random.fold_in(_tk, 500 + 5), (12500, 32), jnp.float32)
        tbl_6 = 0.05 * jax.random.normal(jax.random.fold_in(_tk, 500 + 6), (12500, 32), jnp.float32)
        tbl_7 = 0.05 * jax.random.normal(jax.random.fold_in(_tk, 500 + 7), (125000, 32), jnp.float32)
        tbl_8 = 0.05 * jax.random.normal(jax.random.fold_in(_tk, 500 + 8), (1250, 32), jnp.float32)
        tbl_9 = 0.05 * jax.random.normal(jax.random.fold_in(_tk, 500 + 9), (1250, 32), jnp.float32)
        tbl_10 = 0.05 * jax.random.normal(jax.random.fold_in(_tk, 500 + 10), (1250, 32), jnp.float32)
        tbl_11 = 0.05 * jax.random.normal(jax.random.fold_in(_tk, 500 + 11), (125000, 32), jnp.float32)
        tbl_12 = 0.05 * jax.random.normal(jax.random.fold_in(_tk, 500 + 12), (12500, 32), jnp.float32)
        tbl_13 = 0.05 * jax.random.normal(jax.random.fold_in(_tk, 500 + 13), (12500, 32), jnp.float32)
        tbl_14 = 0.05 * jax.random.normal(jax.random.fold_in(_tk, 500 + 14), (12500, 32), jnp.float32)
        tbl_15 = 0.05 * jax.random.normal(jax.random.fold_in(_tk, 500 + 15), (125000, 32), jnp.float32)
        tbl_16 = 0.05 * jax.random.normal(jax.random.fold_in(_tk, 500 + 16), (1250, 32), jnp.float32)
        tbl_17 = 0.05 * jax.random.normal(jax.random.fold_in(_tk, 500 + 17), (125000, 32), jnp.float32)
        tbl_18 = 0.05 * jax.random.normal(jax.random.fold_in(_tk, 500 + 18), (1000, 32), jnp.float32)
        tbl_19 = 0.05 * jax.random.normal(jax.random.fold_in(_tk, 500 + 19), (125000, 32), jnp.float32)
        tbl_20 = 0.05 * jax.random.normal(jax.random.fold_in(_tk, 500 + 20), (1000, 32), jnp.float32)
        tbl_21 = 0.05 * jax.random.normal(jax.random.fold_in(_tk, 500 + 21), (1250, 32), jnp.float32)
        tbl_22 = 0.05 * jax.random.normal(jax.random.fold_in(_tk, 500 + 22), (12500, 32), jnp.float32)
        tbl_23 = 0.05 * jax.random.normal(jax.random.fold_in(_tk, 500 + 23), (1250, 32), jnp.float32)
        tbl_24 = 0.05 * jax.random.normal(jax.random.fold_in(_tk, 500 + 24), (1250, 32), jnp.float32)
        tbl_25 = 0.05 * jax.random.normal(jax.random.fold_in(_tk, 500 + 25), (125000, 32), jnp.float32)
        tbl_26 = 0.05 * jax.random.normal(jax.random.fold_in(_tk, 500 + 26), (1250, 32), jnp.float32)
        tbl_27 = 0.05 * jax.random.normal(jax.random.fold_in(_tk, 500 + 27), (12500, 32), jnp.float32)
        tbl_28 = 0.05 * jax.random.normal(jax.random.fold_in(_tk, 500 + 28), (1000, 32), jnp.float32)
        tbl_29 = 0.05 * jax.random.normal(jax.random.fold_in(_tk, 500 + 29), (12500, 32), jnp.float32)
        tbl_30 = 0.05 * jax.random.normal(jax.random.fold_in(_tk, 500 + 30), (1250, 32), jnp.float32)
        tbl_31 = 0.05 * jax.random.normal(jax.random.fold_in(_tk, 500 + 31), (1000, 32), jnp.float32)
        tbl_32 = 0.05 * jax.random.normal(jax.random.fold_in(_tk, 500 + 32), (12500, 32), jnp.float32)
        tbl_33 = 0.05 * jax.random.normal(jax.random.fold_in(_tk, 500 + 33), (12500, 32), jnp.float32)
        tbl_34 = 0.05 * jax.random.normal(jax.random.fold_in(_tk, 500 + 34), (1250, 32), jnp.float32)
        tbl_35 = 0.05 * jax.random.normal(jax.random.fold_in(_tk, 500 + 35), (12500, 32), jnp.float32)
        tbl_36 = 0.05 * jax.random.normal(jax.random.fold_in(_tk, 500 + 36), (1000, 32), jnp.float32)
        tbl_37 = 0.05 * jax.random.normal(jax.random.fold_in(_tk, 500 + 37), (1250, 32), jnp.float32)
        tbl_38 = 0.05 * jax.random.normal(jax.random.fold_in(_tk, 500 + 38), (12500, 32), jnp.float32)
        _rk = jax.random.fold_in(_tk, 7)
        W_top1 = 0.049029 * jax.random.normal(jax.random.fold_in(_tk, 801), (416, 512), jnp.float32)
        W_top2 = 0.0441942 * jax.random.normal(jax.random.fold_in(_tk, 802), (512, 256), jnp.float32)
        W_top3 = 0.0625 * jax.random.normal(jax.random.fold_in(_tk, 803), (256, 1), jnp.float32)
        b_top1 = jnp.zeros((512,), jnp.float32)
        b_top2 = jnp.zeros((256,), jnp.float32)
        return (dense_ctx, ids, tbl_0, tbl_1, tbl_2, tbl_3, tbl_4, tbl_5, tbl_6, tbl_7, tbl_8, tbl_9, tbl_10, tbl_11, tbl_12, tbl_13, tbl_14, tbl_15, tbl_16, tbl_17, tbl_18, tbl_19, tbl_20, tbl_21, tbl_22, tbl_23, tbl_24, tbl_25, tbl_26, tbl_27, tbl_28, tbl_29, tbl_30, tbl_31, tbl_32, tbl_33, tbl_34, tbl_35, tbl_36, tbl_37, tbl_38, W_top1, b_top1, W_top2, b_top2, W_top3)
    dense_ctx, ids, tbl_0, tbl_1, tbl_2, tbl_3, tbl_4, tbl_5, tbl_6, tbl_7, tbl_8, tbl_9, tbl_10, tbl_11, tbl_12, tbl_13, tbl_14, tbl_15, tbl_16, tbl_17, tbl_18, tbl_19, tbl_20, tbl_21, tbl_22, tbl_23, tbl_24, tbl_25, tbl_26, tbl_27, tbl_28, tbl_29, tbl_30, tbl_31, tbl_32, tbl_33, tbl_34, tbl_35, tbl_36, tbl_37, tbl_38, W_top1, b_top1, W_top2, b_top2, W_top3 = _rec_inputs()

    def _L0_rec_setup():
        import jax, jax.numpy as jnp
        import numpy as np
        LAYER_SIZE = [200, 200, 200]
        SPLIT_HALF = True
        key = jax.random.key(seed)
        ks = jax.random.split(key, 8)
        B, F0, D = (256, 39, 32)
        field_nums = [F0]
        for i, s in enumerate(LAYER_SIZE):
            field_nums.append(s // 2 if SPLIT_HALF and i != len(LAYER_SIZE) - 1 else s)
        inp = {'x': jax.random.normal(ks[0], (B, F0, D), dtype=jnp.float32)}
        for i, s in enumerate(LAYER_SIZE):
            fan_in = field_nums[i] * F0
            scale = float(np.sqrt(6.0 / (fan_in + s)))
            inp[f'W{i}'] = jax.random.uniform(ks[1 + i], (fan_in, s), dtype=jnp.float32, minval=-scale, maxval=scale)
            inp[f'b{i}'] = jnp.zeros((s,), dtype=jnp.float32)
        return inp
    _L0_rec_all = _L0_rec_setup()
    _L0_rec_in = {k: v for k, v in _L0_rec_all.items() if k in ('W0', 'W1', 'W2', 'b0', 'b1', 'b2')}
    del _L0_rec_all
    return {'dense_ctx': dense_ctx, 'ids': ids, 'tbl_0': tbl_0, 'tbl_1': tbl_1, 'tbl_2': tbl_2, 'tbl_3': tbl_3, 'tbl_4': tbl_4, 'tbl_5': tbl_5, 'tbl_6': tbl_6, 'tbl_7': tbl_7, 'tbl_8': tbl_8, 'tbl_9': tbl_9, 'tbl_10': tbl_10, 'tbl_11': tbl_11, 'tbl_12': tbl_12, 'tbl_13': tbl_13, 'tbl_14': tbl_14, 'tbl_15': tbl_15, 'tbl_16': tbl_16, 'tbl_17': tbl_17, 'tbl_18': tbl_18, 'tbl_19': tbl_19, 'tbl_20': tbl_20, 'tbl_21': tbl_21, 'tbl_22': tbl_22, 'tbl_23': tbl_23, 'tbl_24': tbl_24, 'tbl_25': tbl_25, 'tbl_26': tbl_26, 'tbl_27': tbl_27, 'tbl_28': tbl_28, 'tbl_29': tbl_29, 'tbl_30': tbl_30, 'tbl_31': tbl_31, 'tbl_32': tbl_32, 'tbl_33': tbl_33, 'tbl_34': tbl_34, 'tbl_35': tbl_35, 'tbl_36': tbl_36, 'tbl_37': tbl_37, 'tbl_38': tbl_38, 'W_top1': W_top1, 'b_top1': b_top1, 'W_top2': W_top2, 'b_top2': b_top2, 'W_top3': W_top3, 'L0_rec_W0': _L0_rec_in['W0'], 'L0_rec_W1': _L0_rec_in['W1'], 'L0_rec_W2': _L0_rec_in['W2'], 'L0_rec_b0': _L0_rec_in['b0'], 'L0_rec_b1': _L0_rec_in['b1'], 'L0_rec_b2': _L0_rec_in['b2']}

def reference(dense_ctx, ids, tbl_0, tbl_1, tbl_2, tbl_3, tbl_4, tbl_5, tbl_6, tbl_7, tbl_8, tbl_9, tbl_10, tbl_11, tbl_12, tbl_13, tbl_14, tbl_15, tbl_16, tbl_17, tbl_18, tbl_19, tbl_20, tbl_21, tbl_22, tbl_23, tbl_24, tbl_25, tbl_26, tbl_27, tbl_28, tbl_29, tbl_30, tbl_31, tbl_32, tbl_33, tbl_34, tbl_35, tbl_36, tbl_37, tbl_38, W_top1, b_top1, W_top2, b_top2, W_top3, L0_rec_W0, L0_rec_W1, L0_rec_W2, L0_rec_b0, L0_rec_b1, L0_rec_b2):
    import jax
    import jax.numpy as jnp

    def _L0_rec_ref(x, W0, W1, W2, b0, b1, b2):
        import jax, jax.numpy as jnp
        import numpy as np
        LAYER_SIZE = [200, 200, 200]
        SPLIT_HALF = True
        Ws = [W0, W1, W2]
        bs = [b0, b1, b2]
        B, F0, D = x.shape
        hidden = x
        finals = []
        n_layers = len(LAYER_SIZE)
        for i in range(n_layers):
            z = jnp.einsum('bmd,bnd->bmnd', x, hidden).reshape(B, -1, D)
            cur = jnp.einsum('bcd,co->bod', z, Ws[i]) + bs[i][None, :, None]
            cur = jax.nn.relu(cur)
            if SPLIT_HALF and i != n_layers - 1:
                half = LAYER_SIZE[i] // 2
                hidden, direct = (cur[:, :half, :], cur[:, half:, :])
            else:
                direct = cur
                hidden = cur
            finals.append(direct)
        result = jnp.concatenate(finals, axis=1)
        return jnp.sum(result, axis=-1)
    e = jnp.stack([tbl_0[ids[:, 0]], tbl_1[ids[:, 1]], tbl_2[ids[:, 2]], tbl_3[ids[:, 3]], tbl_4[ids[:, 4]], tbl_5[ids[:, 5]], tbl_6[ids[:, 6]], tbl_7[ids[:, 7]], tbl_8[ids[:, 8]], tbl_9[ids[:, 9]], tbl_10[ids[:, 10]], tbl_11[ids[:, 11]], tbl_12[ids[:, 12]], tbl_13[ids[:, 13]], tbl_14[ids[:, 14]], tbl_15[ids[:, 15]], tbl_16[ids[:, 16]], tbl_17[ids[:, 17]], tbl_18[ids[:, 18]], tbl_19[ids[:, 19]], tbl_20[ids[:, 20]], tbl_21[ids[:, 21]], tbl_22[ids[:, 22]], tbl_23[ids[:, 23]], tbl_24[ids[:, 24]], tbl_25[ids[:, 25]], tbl_26[ids[:, 26]], tbl_27[ids[:, 27]], tbl_28[ids[:, 28]], tbl_29[ids[:, 29]], tbl_30[ids[:, 30]], tbl_31[ids[:, 31]], tbl_32[ids[:, 32]], tbl_33[ids[:, 33]], tbl_34[ids[:, 34]], tbl_35[ids[:, 35]], tbl_36[ids[:, 36]], tbl_37[ids[:, 37]], tbl_38[ids[:, 38]]], axis=1)
    z = _L0_rec_ref(e, L0_rec_W0, L0_rec_W1, L0_rec_W2, L0_rec_b0, L0_rec_b1, L0_rec_b2)
    z = z.reshape(z.shape[0], -1)
    h = jnp.concatenate([z, dense_ctx], axis=1)
    h = jnp.maximum(h @ W_top1 + b_top1, 0.0)
    h = jnp.maximum(h @ W_top2 + b_top2, 0.0)
    y = h @ W_top3
    return y

_drawn_inputs = setup_inputs


def setup_inputs(seed=0):
    import zlib

    import numpy as np

    out = dict(_drawn_inputs(seed))
    spreads = {'b_top1': (0.0, 2.0),
     'b_top2': (0.0, 2.0),
     'L0_rec_b0': (0.0, 0.604),
     'L0_rec_b1': (0.0, 0.8),
     'L0_rec_b2': (0.0, 2.0)}
    factors = {'tbl_0': 8.0,
     'tbl_1': 8.0,
     'tbl_2': 8.0,
     'tbl_3': 8.0,
     'tbl_4': 8.0,
     'tbl_5': 8.0,
     'tbl_6': 8.0,
     'tbl_7': 8.0,
     'tbl_8': 8.0,
     'tbl_9': 8.0,
     'tbl_10': 8.0,
     'tbl_11': 8.0,
     'tbl_12': 8.0,
     'tbl_13': 8.0,
     'tbl_14': 8.0,
     'tbl_15': 8.0,
     'tbl_16': 8.0,
     'tbl_17': 8.0,
     'tbl_18': 8.0,
     'tbl_19': 8.0,
     'tbl_20': 8.0,
     'tbl_21': 8.0,
     'tbl_22': 8.0,
     'tbl_23': 8.0,
     'tbl_24': 8.0,
     'tbl_25': 8.0,
     'tbl_26': 8.0,
     'tbl_27': 8.0,
     'tbl_28': 8.0,
     'tbl_29': 8.0,
     'tbl_30': 8.0,
     'tbl_31': 8.0,
     'tbl_32': 8.0,
     'tbl_33': 8.0,
     'tbl_34': 8.0,
     'tbl_35': 8.0,
     'tbl_36': 8.0,
     'tbl_37': 8.0,
     'tbl_38': 8.0,
     'L0_rec_W0': 8.0,
     'L0_rec_W1': 7.306,
     'L0_rec_W2': 4.702,
     'dense_ctx': 32.832}
    for name, (base, spread) in spreads.items():
        noise = np.random.default_rng([zlib.crc32(name.encode()), seed]).standard_normal(out[name].shape)
        drawn = base * np.exp(spread * noise) if base else spread * noise
        out[name] = jnp.asarray(drawn.astype(out[name].dtype))
    for name, factor in factors.items():
        out[name] = (out[name] * factor).astype(out[name].dtype)
    return out
```

```python
B, F, D, DENSE = 512, 39, 32, 16
P = 128
UNITS, HALF = 200, 100
CHUNKS = B // P
DB = 2
COLS = DB * P
BLOCKS = CHUNKS * D // DB
MG, NGRP = 5, 25
KT = MG * NGRP
J = (F + MG - 1) // MG
G = HALF // NGRP
KLAST = (F - MG * (J - 1)) * NGRP
SHIFTS = (F + 1) // 2
SPT = 3
K0 = SPT * F
T0 = (SHIFTS + SPT - 1) // SPT
K0LAST = (SHIFTS - SPT * (T0 - 1)) * F
PARTS = 3 * F + 1
TG = 4
QA = J * G // TG
QB = (T0 + TG - 1) // TG
OFFSETS = 2 * QA + QB
TILES = T0 + 2 * J * G
ZF_SLOTS, ZH_SLOTS, ZL_SLOTS = 3, 4, 3
SUB_D = 8
SUB_BLOCKS = SUB_D // DB
SUBS = D // SUB_D

SUM_A_AT, SUM_B_AT, SUM_C_AT = 12, 14, 4
HE_LEAD = 3
ZL_LAG = 2
XT_COPY_AT, A3_COPY_AT, XB_COPY_AT = 5, 6, 12
HR_LEAD = 5
TENSOR_FILLS = {0: ("T",), 1: ("A3",), 2: (0,), 3: (1,), 4: (2,), 5: (3,),
                8: ("X0",), 9: ("X1",), 10: ("X2",), 11: ("X3",)}
POOL_LOW = {0, 2, 4, 6, 7, 9, 11, 13, 15, 17}


def offset_of(kind, q):
    return {"A": 0, "B": QA, "C": QA + QB}[kind] + q


def kind_at(o):
    if o < QA:
        return "A", o
    if o < QA + QB:
        return "B", o - QA
    return "C", o - QA - QB


def exists(kind, i):
    return {"A": 0 <= i <= BLOCKS - 1, "B": -1 <= i <= BLOCKS - 2, "C": 1 <= i <= BLOCKS}[kind]


def build_counts():
    z, low_pool, low_dve, hr, order = {}, {}, {}, {}, []
    for i in range(-1, BLOCKS + 1):
        for o in range(OFFSETS):
            kind, q = kind_at(o)
            if not exists(kind, i):
                continue
            z[kind, i, q] = len(z) + 1
            if o in POOL_LOW:
                low_pool[kind, i, q] = len(low_pool) + 1
            else:
                low_dve[kind, i, q] = len(low_dve) + 1
            if kind != "B" and q % 2 == 0:
                hr[kind, i, q // 2] = len(hr) + 1
                order.append((kind, i, q // 2))
    return z, low_pool, low_dve, hr, order


def build(nc, ids, tables, w0_direct, w0_swapped, w1, w2, sel_in, identity_in, w_top1, w_top1_dense,
          b_top1, w_top2, b_top2, w_top3, dense_t, out):
    import concourse.bass as bass
    from concourse import mybir
    from contextlib import ExitStack

    f32, f32r = mybir.dt.float32, mybir.dt.float32r
    bf16, i32 = mybir.dt.bfloat16, mybir.dt.int32
    ALU, ACT = mybir.AluOpType, mybir.ActivationFunctionType

    Z, LOWP, LOWD, HRN, HR_ORDER = build_counts()
    N_GRANULES = len(Z)
    POOL_SET = set(LOWP)

    class Step:

        def __init__(self, rep, expr=None):
            self.rep, self.expr = rep, expr

        def has(self, kind, di=0):
            return exists(kind, self.rep + di)

        def count(self, f):
            if self.expr is None:
                return f(self.rep)
            slope = (f(self.rep + 6) - f(self.rep)) // 6
            return self.expr * slope + (f(self.rep) - slope * self.rep)

    def run_steps(engine, step, first, unroll, last=BLOCKS + 1):
        for i in range(-1, first):
            step(Step(i))
        assert (BLOCKS - 1 - first) % unroll == 0
        with engine.Fori(0, (BLOCKS - 1 - first) // unroll) as turn:
            for k in range(unroll):
                step(Step(first + k, turn * unroll + (first + k)))
        for i in range(BLOCKS - 1, last + 1):
            step(Step(i))

    with ExitStack() as ctx:
        def sb(name, shape, dt=f32):
            return ctx.enter_context(nc.sbuf_tensor(name, shape, dt))

        def sem(name):
            return ctx.enter_context(nc.semaphore(name))

        weights = sb("weights", [P, TILES, 2 * UNITS], f32r)
        xb = sb("x_repeated", [P, 3, J, COLS])
        zf = sb("z_full", [P, ZF_SLOTS, TG, COLS])
        zh = sb("z_high", [P, ZH_SLOTS, TG, COLS], f32r)
        zl = sb("z_low", [P, ZL_SLOTS, TG, COLS], f32r)
        a3 = sb("x_three_times", [P, COLS])
        sel = sb("selection", [P, J + 1 + T0, KT], bf16)
        xt3 = sb("x_parts_transposed", [P, COLS], bf16)
        px = sb("x_parts", [P, 2, DB * PARTS], bf16)
        sum_a = sb("sum_a", [P, 2, DB, UNITS])
        sum_bc = sb("sum_bc", [P, DB, UNITS])
        he = sb("hidden_repeated", [P, 2, DB, KT])
        pooled = sb("pooled", [P, CHUNKS, 2 * UNITS])
        ident = sb("ident", [P, P])
        identb = sb("identb", [P, P], bf16)
        xg = sb("x_gathered", [P, F, D])
        p3 = sb("x_split", [P, SUB_BLOCKS, DB * PARTS], bf16)
        idx = sb("idx", [P, CHUNKS, F], i32)
        parts_dram = nc.dram_tensor("x_parts_dram", [BLOCKS, P, DB * PARTS], bf16, kind="Internal").ap()

        acc = [ctx.enter_context(nc.psum_tensor(f"acc{s}", [P, DB, 512], f32)) for s in range(2)]
        hr_ps = ctx.enter_context(nc.psum_tensor("hr_ps", [P, 2, 512], f32))
        sel_ps = ctx.enter_context(nc.psum_tensor("sel_ps", [P, 2, 512], f32))

        xb_flat = xb[:, :, :, :].rearrange("p a j c -> p (a j c)")
        zf_flat = zf[:, :, :, :].rearrange("p a j c -> p (a j c)")
        GW = J * UNITS
        stage = [xb_flat[:, s * GW:(s + 1) * GW].rearrange("p (t o) -> p t o", o=UNITS) for s in range(3)]
        stage.append(zf_flat[:, 0:GW].rearrange("p (t o) -> p t o", o=UNITS))

        w1t = xb_flat[0:HALF, 0:4 * 512].rearrange("p (k n) -> p k n", k=4)
        w2t = xb_flat[:, 2048:3072].rearrange("p (k n) -> p k n", k=4)
        w3t = xb_flat[:, 3072:3074]
        b1t = xb_flat[:, 3074:3078]
        b2t = xb_flat[:, 3078:3080]
        ht = xb_flat[0:HALF, 3080:5128].rearrange("p (k n) -> p k n", k=4)
        h2 = xb_flat[:, 3080:4104].rearrange("p (k n) -> p k n", k=2)
        h1 = zf_flat[:, 0:2048].rearrange("p (k n) -> p k n", k=4)
        denset = zf_flat[0:DENSE, 2048:2560]
        w1d = zf_flat[0:DENSE, 2560:3072]
        y_row = xb_flat[0:1, 5200:5712]

        const_loaded = sem("const_loaded")
        ids_loaded = sem("ids_loaded")
        stage_loaded = [sem(f"stage_loaded{s}") for s in range(4)]
        w_added = sem("w_added")
        w_high = sem("w_high")
        w_low = sem("w_low")
        identb_ready = sem("identb_ready")
        filled = sem("filled")
        pooled_zero = sem("pooled_zero")
        gathered = sem("gathered")
        split_step = sem("split_step")
        parts_stored = sem("parts_stored")
        px_loaded = [sem(f"px_loaded{s}") for s in range(2)]
        sel_done = sem("sel_done")
        sel_copied = sem("sel_copied")
        bt_half = sem("bt_half")
        he_done = sem("he_done")
        hr_done = sem("hr_done")
        z_done = sem("z_done")
        zh_done = sem("zh_done")
        low_pool = sem("low_pool")
        low_dve = sem("low_dve")
        pe_used = sem("pe_used")
        lo_copied = {k: sem(f"lo_copied_{k}") for k in "ABC"}
        sum_done = {k: sem(f"sum_done_{k}") for k in "ABC"}
        pooled_step = sem("pooled_step")
        pooled_done = {k: sem(f"pooled_done_{k}") for k in "ABC"}
        top_loaded = sem("top_loaded")
        top_t = sem("top_t")
        top_copied = sem("top_copied")
        top_mm = sem("top_mm")
        top_act = sem("top_act")
        out_stored = sem("out_stored")

        ended = {"A": lambda i: i + 1, "B": lambda i: i + 2, "C": lambda i: i}

        def phase_set(kind, i):
            return (3 * i + {"A": 1, "B": 2, "C": 3}[kind]) % 2

        def tiles_of(kind, q):
            if kind == "B":
                return [(t - TG * q, t, K0 + 1 if t == 0 else (K0LAST if t == T0 - 1 else K0),
                         K0LAST if t == T0 - 1 else K0) for t in range(TG * q, min(T0, TG * q + TG))]
            base = T0 + (J * G if kind == "C" else 0)
            rows = []
            for u in range(TG):
                j = TG * (q % 2) + u
                k = KLAST if j == J - 1 else KT
                rows.append((u, base + J * (q // 2) + j, KT + 1 if (q, j) == (0, 0) else k, k))
            return rows

        def before(kind, di, q):
            o = offset_of(kind, q) + OFFSETS * di - ZL_LAG
            k, r = kind_at(o % OFFSETS)
            return k, o // OFFSETS, r

        block = ctx.enter_context(nc.Block())

        @block.sync
        def _(sp):
            sp.dma_start(idx[:, :, :], ids).then_inc(ids_loaded, 16)
            sp.dma_start(stage[0][0:K0 + 1, 0:T0, :], w0_direct).then_inc(stage_loaded[0], 16)
            sp.dma_start(stage[1][0:K0 + 1, 0:T0, :], w0_swapped).then_inc(stage_loaded[1], 16)
            sp.dma_start(sel[0:PARTS, :, :], sel_in).then_inc(const_loaded, 16)
            sp.dma_start(ident[:, :], identity_in).then_inc(const_loaded, 16)
            for n in range(2 * G):
                s = (n + 2) % 4
                if n >= 2:
                    sp.wait_ge(w_high, max(1, n - 2))
                    sp.wait_ge(w_low, max(1, n - 2))
                src = (w1, w2)[n // G]
                g = n % G
                sp.dma_start(stage[s][0:KT + 1, 0:J, :], src[:, J * g:J * (g + 1), :]).then_inc(stage_loaded[s], 16)

            def load_parts(i, k):
                sp.dma_start(px[:, k % 2, :], parts_dram[bass.ds(i, 1), :, :].rearrange("k b n -> b (k n)")
                             ).then_inc(px_loaded[k % 2], 16)

            for k in range(4):
                if k == 0:
                    sp.wait_ge(parts_stored, 16)
                if k >= 2:
                    sp.wait_ge(sel_done, 10 * (k - 2) + 1)
                load_parts(k, k)
            with sp.Fori(1, BLOCKS // 4) as turn:
                sp.wait_ge(parts_stored, turn * 16 + 16)
                for k in range(4):
                    sp.wait_ge(sel_done, turn * 40 + (10 * (k - 2) + 1))
                    load_parts(turn * 4 + k, k)

            sp.wait_ge(z_done, N_GRANULES)
            sp.wait_ge(zh_done, N_GRANULES)
            sp.wait_ge(low_pool, len(LOWP))
            sp.wait_ge(low_dve, len(LOWD))
            for dst, src in ((w1t, w_top1), (w1d, w_top1_dense), (denset, dense_t), (b1t, b_top1), (w2t, w_top2),
                             (b2t, b_top2), (w3t, w_top3)):
                sp.dma_start(dst, src).then_inc(top_loaded, 16)
            sp.wait_ge(top_act, 7)
            sp.dma_start(out.rearrange("b o -> o b"), y_row).then_inc(out_stored, 16)
            sp.wait_ge(out_stored, 16)

        @block.gpsimd
        def _(pool):
            chain = [0]

            def link(ins):
                chain[0] += 1
                ins.then_inc(split_step, 1)
                pool.wait_ge(split_step, chain[0])

            def gather(c, fields):
                for f in fields:
                    pool.indirect_dma_start(xg[:, f, :], None, tables[f],
                                            bass.IndirectOffsetOnAxis(idx[:, c, f:f + 1], 0)).then_inc(gathered, 16)

            def split(c, s):
                n = c * SUBS + s
                if n:
                    pool.wait_ge(parts_stored, 16 * n)
                x = xg[:, :, SUB_D * s:SUB_D * (s + 1)]
                parts = p3[:, :, :].rearrange("p k (e n) -> p (k e) n", e=DB)
                for part in range(3):
                    y = parts[:, :, F * part:F * (part + 1)].rearrange("p d f -> p f d")
                    link(pool.tensor_copy(y, x))
                    if part < 2:
                        link(pool.tensor_tensor(x, x, y, ALU.subtract))
                pool.dma_start(parts_dram[n * SUB_BLOCKS:(n + 1) * SUB_BLOCKS, :, :].rearrange("k b n -> b k n"),
                               p3[:, :, :]).then_inc(parts_stored, 16)

            pool.wait_ge(ids_loaded, 16)
            gather(0, range(F))
            link(pool.memset(p3[:, :, :], 1.0))
            pool.wait_ge(gathered, 16 * F)
            for s in range(SUBS):
                split(0, s)

            def low_part(st, kind, di, q):
                z = lambda i: Z[kind, i + di, q]
                slot_of = Z[kind, st.rep + di, q] - 1
                pool.wait_ge(zh_done, st.count(z))
                if Z[kind, st.rep + di, q] > ZL_SLOTS:
                    pool.wait_ge(pe_used, st.count(lambda i: z(i) - ZL_SLOTS))
                n = len(tiles_of(kind, q))
                pool.tensor_tensor(zl[0:KT, slot_of % ZL_SLOTS, 0:n, :], zf[0:KT, slot_of % ZF_SLOTS, 0:n, :],
                                   zh[0:KT, slot_of % ZH_SLOTS, 0:n, :].bitcast(f32),
                                   ALU.subtract).then_inc(low_pool, 1)

            def step(st):
                for o in range(OFFSETS):
                    kind, q = kind_at(o)
                    lk, ldi, lq = before(kind, 0, q)
                    if st.has(lk, ldi) and (lk, st.rep + ldi, lq) in POOL_SET:
                        low_part(st, lk, ldi, lq)
                if st.expr is None and 0 <= st.rep < 5 * (CHUNKS - 1):
                    c, part = st.rep // 5 + 1, st.rep % 5
                    if part < 3:
                        if part == 0:
                            pool.wait_ge(split_step, chain[0])
                        gather(c, range(13 * part, 13 * part + 13))
                    else:
                        pool.wait_ge(gathered, 16 * F * (c + 1))
                        split(c, 2 * (part - 3))
                        split(c, 2 * (part - 3) + 1)

            run_steps(pool, step, 15, 2)
            pool.wait_ge(parts_stored, 16 * CHUNKS * SUBS)

        @block.scalar
        def _(act):
            act.wait_ge(const_loaded, 32)
            act.activation(identb[:, :], ident[:, :], ACT.Copy).then_inc(identb_ready, 1)

            act.wait_ge(w_added, 1)
            act.activation(weights[0:K0 + 1, 0:T0, 0:UNITS], stage[0][0:K0 + 1, 0:T0, :], ACT.Copy).then_inc(w_high, 1)
            for n in range(2 * G):
                s = (n + 2) % 4
                act.wait_ge(stage_loaded[s], 16 * (1 + (n + 2) // 4))
                act.activation(weights[0:KT + 1, T0 + J * n:T0 + J * (n + 1), 0:UNITS], stage[s][0:KT + 1, :, :],
                               ACT.Copy).then_inc(w_high, 1)
            act.wait_ge(w_low, 1 + 2 * G)
            act.wait_ge(filled, 1)

            def high_part(st, kind, q):
                z = lambda i: Z[kind, i, q]
                n0 = Z[kind, st.rep, q]
                act.wait_ge(z_done, st.count(z))
                if n0 > ZH_SLOTS:
                    act.wait_ge(pe_used, st.count(lambda i: z(i) - ZH_SLOTS))
                n = len(tiles_of(kind, q))
                act.activation(zh[0:KT, (n0 - 1) % ZH_SLOTS, 0:n, :], zf[0:KT, (n0 - 1) % ZF_SLOTS, 0:n, :],
                               ACT.Copy).then_inc(zh_done, 1)

            def copy_small(st, kind, di):
                if not st.has(kind, di):
                    return
                i = st.rep + di
                act.wait_ge(pe_used, st.count(lambda i: Z[kind, i + di, (QB if kind == "B" else QA) - 1]))
                if kind == "A":
                    dst = sum_a[:, i % 2, :, :]
                    if i >= 2:
                        act.wait_ge(pooled_done["A"], st.count(lambda i: ended["A"](i + di - 2)))
                        act.wait_ge(he_done, st.count(lambda i: HRN["C", i + di - 1, G - 1]))
                elif kind == "B":
                    dst = sum_bc[:, :, :]
                    if i >= 2:
                        act.wait_ge(pooled_done["C"], st.count(lambda i: ended["C"](i + di - 1)))
                    elif i >= 0:
                        act.wait_ge(pooled_done["B"], ended["B"](i - 1))
                        act.wait_ge(he_done, HRN["A", i, G - 1])
                else:
                    dst = sum_bc[:, :, :]
                    act.wait_ge(pooled_done["B"], st.count(lambda i: min(ended["B"](i + di), BLOCKS)))
                    if exists("A", i + 1):
                        act.wait_ge(he_done, st.count(lambda i: HRN["A", i + di + 1, G - 1]))
                act.activation(dst, acc[phase_set(kind, i)][:, :, UNITS:2 * UNITS], ACT.Copy).then_inc(lo_copied[kind], 1)

            def repeat_hidden(st, kind, di, g):
                if not st.has(kind, di):
                    return
                i = st.rep + di
                n0 = HRN[kind, i, g]
                if kind == "A":
                    act.wait_ge(sum_done["B"], st.count(lambda i: ended["B"](i + di - 1)))
                    v = sum_bc[:, :, NGRP * g:NGRP * (g + 1)]
                else:
                    act.wait_ge(sum_done["A"], st.count(lambda i: ended["A"](i + di - 1)))
                    v = sum_a[:, (i - 1) % 2, :, NGRP * g:NGRP * (g + 1)]
                if n0 > 2:
                    act.wait_ge(hr_done, st.count(lambda i: HRN[kind, i + di, g] - 2))
                act.activation(he[:, g % 2, :, :].rearrange("p e (r n) -> p e r n", r=MG),
                               v.unsqueeze(2).to_broadcast([P, DB, MG, NGRP]), ACT.Relu).then_inc(he_done, 1)

            def copy_parts(st):
                if st.has("B"):
                    act.wait_ge(sel_done, st.count(lambda i: 10 * (i + 1) + 1))
                    act.activation(xt3[0:PARTS, :], sel_ps[0:PARTS, 0, 0:COLS // 2].bitcast(bf16),
                                   ACT.Copy).then_inc(sel_copied, 1)

            def copy_a3(st):
                if st.has("B"):
                    act.wait_ge(sel_done, st.count(lambda i: 10 * (i + 1) + 2))
                    if st.rep >= 0:
                        act.wait_ge(z_done, st.count(lambda i: Z["B", i - 1, QB - 1]))
                    act.activation(a3[0:KT, :], sel_ps[0:KT, 1, 0:COLS], ACT.Copy).then_inc(sel_copied, 1)

            def copy_xb(st, k):
                if st.has("B"):
                    b = st.rep + 1
                    act.wait_ge(sel_done, st.count(lambda i: 10 * (i + 1) + 7 + k))
                    if b >= 3:
                        act.wait_ge(z_done, st.count(lambda i: Z["C", i - 1, QA - 1]))
                    act.activation(xb[0:KT, b % 3, 2 * k:2 * k + 2, :].rearrange("p j c -> p (j c)"),
                                   sel_ps[0:KT, k % 2, :], ACT.Copy).then_inc(sel_copied, 1)

            def step(st):
                for o in range(OFFSETS):
                    if o == SUM_C_AT:
                        copy_small(st, "C", -1)
                    if o == SUM_A_AT:
                        copy_small(st, "A", 0)
                    if o == SUM_B_AT:
                        copy_small(st, "B", 0)
                    if o == XT_COPY_AT:
                        copy_parts(st)
                    if o == A3_COPY_AT:
                        copy_a3(st)
                    if XB_COPY_AT <= o < XB_COPY_AT + 4:
                        copy_xb(st, o - XB_COPY_AT)
                    for kind, di in (("A", 0), ("C", 0), ("A", 1)):
                        for g in range(G):
                            if offset_of(kind, 2 * g) + OFFSETS * di - HE_LEAD == o:
                                repeat_hidden(st, kind, di, g)
                    kind, q = kind_at(o)
                    if st.has(kind):
                        high_part(st, kind, q)

            run_steps(act, step, 3, 6)

            for k in range(4):
                act.wait_ge(top_t, k + 1)
                if k == 0:
                    act.wait_ge(z_done, N_GRANULES)
                src = (hr_ps, sel_ps)[k // 2][0:HALF, k % 2, :]
                act.activation(ht[:, k, :], src, ACT.Copy).then_inc(top_copied, 1)
            act.wait_ge(top_loaded, 7 * 16)
            act.wait_ge(low_pool, len(LOWP))
            act.wait_ge(low_dve, len(LOWD))
            for m in range(4):
                act.wait_ge(top_mm, m + 1)
                act.activation(h1[:, m, :], acc[m // 2][:, m % 2, :], ACT.Relu, bias=b1t[:, m:m + 1]).then_inc(top_act, 1)
            for m in range(2):
                act.wait_ge(top_mm, 5 + m)
                act.activation(h2[:, m, :], hr_ps[:, m, :], ACT.Relu, bias=b2t[:, m:m + 1]).then_inc(top_act, 1)
            act.wait_ge(top_mm, 7)
            act.activation(y_row, sel_ps[0:1, 0, :], ACT.Copy).then_inc(top_act, 1)

        @block.vector
        def _(dve):
            dve.memset(zh[:, :, :, :].bitcast(f32), 1.0).then_inc(filled, 1)
            dve.memset(pooled[:, :, :], 0.0).then_inc(pooled_zero, 1)
            dve.wait_ge(stage_loaded[0], 16)
            dve.wait_ge(stage_loaded[1], 16)
            s0, s1 = stage[0][0:K0 + 1, 0:T0, :], stage[1][0:K0 + 1, 0:T0, :]
            dve.tensor_tensor(s0, s0, s1, ALU.add).then_inc(w_added, 1)
            dve.wait_ge(w_high, 1)
            dve.tensor_tensor(weights[0:K0 + 1, 0:T0, UNITS:2 * UNITS], s0,
                              weights[0:K0 + 1, 0:T0, 0:UNITS].bitcast(f32), ALU.subtract).then_inc(w_low, 1)
            for n in range(2 * G):
                w = weights[0:KT + 1, T0 + J * n:T0 + J * (n + 1), :]
                dve.wait_ge(w_high, n + 2)
                dve.tensor_tensor(w[:, :, UNITS:2 * UNITS], stage[(n + 2) % 4][0:KT + 1, :, :],
                                  w[:, :, 0:UNITS].bitcast(f32), ALU.subtract).then_inc(w_low, 1)
            dve.wait_ge(pooled_zero, 1)
            pooled_steps = [0]

            def product(st, kind, q):
                z = lambda i: Z[kind, i, q]
                n0 = Z[kind, st.rep, q]
                slot = (n0 - 1) % ZF_SLOTS
                if n0 > ZF_SLOTS:
                    was = [key for key, value in Z.items() if value == n0 - ZF_SLOTS][0]
                    wk, wi, wq = was
                    di = wi - st.rep
                    if was in POOL_SET:
                        dve.wait_ge(low_pool, st.count(lambda i: LOWP[wk, i + di, wq]))
                    else:
                        dve.wait_ge(low_dve, st.count(lambda i: LOWD[wk, i + di, wq]))
                if kind == "B":
                    for h in range(2):
                        fill = 2 * q + h
                        n = min(2, T0 - 2 * fill)
                        dve.wait_ge(sel_done, st.count(lambda i: 10 * (i + 1) + 3 + fill))
                        if fill == 0:
                            dve.wait_ge(sel_copied, st.count(lambda i: 6 * (i + 1) + 2))
                        ins = dve.tensor_tensor(
                            zf[0:KT, slot, 2 * h:2 * h + n, :],
                            a3[0:KT, :].unsqueeze(1).to_broadcast([KT, n, COLS]),
                            sel_ps[0:KT, fill % 2, 0:n * COLS].rearrange("p (t c) -> p t c", t=n), ALU.mult)
                        ins.then_inc((bt_half, z_done)[h], 1)
                    return
                b = st.rep if kind == "A" else st.rep - 1
                if q == 0 and kind == "A":
                    dve.wait_ge(sel_copied, st.count(lambda i: 6 * i + 6))
                if q % 2 == 0:
                    dve.wait_ge(hr_done, st.count(lambda i: HRN[kind, i, q // 2]))
                j0 = TG * (q % 2)
                dve.tensor_tensor(zf[0:KT, slot, :, :], xb[0:KT, b % 3, j0:j0 + TG, :],
                                  hr_ps[0:KT, (q // 2) % 2, 0:COLS].unsqueeze(1).to_broadcast([KT, TG, COLS]),
                                  ALU.mult).then_inc(z_done, 1)

            def low_part(st, kind, di, q):
                z = lambda i: Z[kind, i + di, q]
                n0 = Z[kind, st.rep + di, q]
                dve.wait_ge(zh_done, st.count(z))
                if n0 > ZL_SLOTS:
                    dve.wait_ge(pe_used, st.count(lambda i: z(i) - ZL_SLOTS))
                n = len(tiles_of(kind, q))
                dve.tensor_tensor(zl[0:KT, (n0 - 1) % ZL_SLOTS, 0:n, :], zf[0:KT, (n0 - 1) % ZF_SLOTS, 0:n, :],
                                  zh[0:KT, (n0 - 1) % ZH_SLOTS, 0:n, :].bitcast(f32),
                                  ALU.subtract).then_inc(low_dve, 1)

            def add_and_pool(st, kind, di):
                if not st.has(kind, di):
                    return
                i = st.rep + di
                dst = sum_a[:, i % 2, :, :] if kind == "A" else sum_bc[:, :, :]
                dve.wait_ge(lo_copied[kind], st.count(lambda i: ended[kind](i + di)))
                dve.tensor_tensor(dst, acc[phase_set(kind, i)][:, :, 0:UNITS], dst, ALU.add).then_inc(sum_done[kind], 1)
                first = 0 if kind == "C" else HALF
                units = UNITS - first
                at = {"B": 0, "A": HALF, "C": 2 * HALF}[kind]
                db = {"A": 0, "B": 1, "C": -1}[kind] + di
                if st.expr is None:
                    c = (st.rep + db) // (BLOCKS // CHUNKS)
                    total = pooled[:, c, at:at + units]
                else:
                    c = (st.expr + db) // (BLOCKS // CHUNKS)
                    total = pooled[:, bass.ds(c, 1), at:at + units].rearrange("p c n -> p (c n)")
                dve.wait_ge(sum_done[kind], st.count(lambda i: ended[kind](i + di)))
                dve.scalar_tensor_tensor(total, dst[:, 0, first:UNITS], 0.0, total, ALU.max, ALU.add
                                         ).then_inc(pooled_step, 1)
                dve.wait_ge(pooled_step, st.count(lambda i: steps_before(i + di, kind) + 1))
                dve.scalar_tensor_tensor(total, dst[:, 1, first:UNITS], 0.0, total, ALU.max, ALU.add
                                         ).then_inc(pooled_done[kind], 1)

            def steps_before(i, kind):
                order = []
                for s in range(-1, BLOCKS + 2):
                    for k, di, o in (("C", -1, SUM_C_AT), ("A", 0, SUM_A_AT), ("B", 0, SUM_B_AT)):
                        if exists(k, s + di):
                            order.append((k, s + di))
                return order.index((kind, i))

            def step(st):
                for o in range(OFFSETS):
                    if o == SUM_C_AT:
                        add_and_pool(st, "C", -1)
                    if o == SUM_A_AT:
                        add_and_pool(st, "A", 0)
                    if o == SUM_B_AT:
                        add_and_pool(st, "B", 0)
                    kind, q = kind_at(o)
                    lk, ldi, lq = before(kind, 0, q)
                    if st.has(lk, ldi) and (lk, st.rep + ldi, lq) not in POOL_SET:
                        low_part(st, lk, ldi, lq)
                    if st.has(kind):
                        product(st, kind, q)

            run_steps(dve, step, 3, 6)

        @block.tensor
        def _(pe):
            pe.wait_ge(identb_ready, 1)
            pe.wait_ge(w_low, 1 + 2 * G)

            def hidden_fill(st, kind, di, g):
                if not st.has(kind, di):
                    return
                n0 = HRN[kind, st.rep + di, g]
                pe.wait_ge(he_done, st.count(lambda i: HRN[kind, i + di, g]))
                if n0 > 2:
                    wk, wi, wg = HR_ORDER[n0 - 3]
                    wdi = wi - st.rep
                    pe.wait_ge(z_done, st.count(lambda i: Z[wk, i + wdi, 2 * wg + 1]))
                for e in range(DB):
                    last = pe.matmul(hr_ps[0:KT, g % 2, e * P:(e + 1) * P], he[:, g % 2, e, :], ident[:, :],
                                     start=True, stop=True, is_transpose=True)
                last.then_inc(hr_done, 1)

            def select(bank, half, which):
                return pe.matmul(sel_ps[0:KT, bank, half * COLS:(half + 1) * COLS], sel[0:PARTS, which, :],
                                 xt3[0:PARTS, :], start=True, stop=True)

            def tensor_fill(st, what):
                if not st.has("B"):
                    return
                b = st.rep + 1
                if what == "T":
                    pe.wait_ge(px_loaded[b % 2], st.count(lambda i: 16 * ((i + 1) // 2 + 1)))
                    if b >= 1:
                        pe.wait_ge(sel_copied, st.count(lambda i: 6 * i + 5))
                    for e in range(DB):
                        last = pe.transpose(sel_ps[0:PARTS, 0, e * P // 2:(e + 1) * P // 2].bitcast(bf16),
                                            px[:, b % 2, e * PARTS:(e + 1) * PARTS], identb[:, :])
                    last.then_inc(sel_done, 1)
                    return
                if what == "A3":
                    pe.wait_ge(sel_copied, st.count(lambda i: 6 * (i + 1) + 1))
                    select(1, 0, J).then_inc(sel_done, 1)
                    return
                if what in (0, 1, 2, 3):
                    if what == 1:
                        pe.wait_ge(sel_copied, st.count(lambda i: 6 * (i + 1) + 2))
                    if what == 2:
                        pe.wait_ge(bt_half, st.count(lambda i: 2 * (i + 1) + 1))
                    if what == 3:
                        pe.wait_ge(z_done, st.count(lambda i: Z["B", i, 0]))
                    for h in range(min(2, T0 - 2 * what)):
                        last = select(what % 2, h, J + 1 + 2 * what + h)
                    last.then_inc(sel_done, 1)
                    return
                k = int(what[1])
                if k == 0:
                    pe.wait_ge(bt_half, st.count(lambda i: 2 * (i + 1) + 2))
                elif k == 1:
                    pe.wait_ge(z_done, st.count(lambda i: Z["B", i, 1]))
                else:
                    pe.wait_ge(sel_copied, st.count(lambda i: 6 * (i + 1) + 1 + k))
                for h in range(2):
                    last = select(k % 2, h, 2 * k + h)
                last.then_inc(sel_done, 1)

            def granule(st, kind, q):
                i = st.rep
                if q == 0:
                    if kind == "A":
                        pe.wait_ge(sum_done["B"], st.count(lambda i: ended["B"](i - 1)))
                    elif kind == "B" and i >= 2:
                        pe.wait_ge(sum_done["C"], st.count(lambda i: ended["C"](i - 1)))
                    elif kind == "B" and i == 1:
                        pe.wait_ge(sum_done["A"], 1)
                    elif kind == "C" and i < BLOCKS:
                        pe.wait_ge(sum_done["A"], st.count(ended["A"]))
                    elif kind == "C":
                        pe.wait_ge(sum_done["C"], BLOCKS - 2)
                z = lambda i: Z[kind, i, q]
                n0 = Z[kind, i, q] - 1
                key = (kind, i, q)
                pe.wait_ge(zh_done, st.count(z))
                if key in POOL_SET:
                    pe.wait_ge(low_pool, st.count(lambda i: LOWP[kind, i, q]))
                else:
                    pe.wait_ge(low_dve, st.count(lambda i: LOWD[kind, i, q]))
                phase = acc[phase_set(kind, i)]
                last_q = q == (QB if kind == "B" else QA) - 1
                tiles = tiles_of(kind, q)
                for e in range(DB):
                    for u, w, k_high, k_low in tiles:
                        high = zh[0:k_high, n0 % ZH_SLOTS, u, e * P:(e + 1) * P]
                        low = zl[0:k_low, n0 % ZL_SLOTS, u, e * P:(e + 1) * P]
                        pe.matmul(phase[:, e, 0:2 * UNITS], high, weights[0:k_high, w, :],
                                  start=(q == 0 and u == 0), stop=False)
                        last = pe.matmul(phase[:, e, UNITS:2 * UNITS], low, weights[0:k_low, w, 0:UNITS],
                                         start=False, stop=(last_q and u == len(tiles) - 1))
                last.then_inc(pe_used, 1)

            def step(st):
                for o in range(OFFSETS):
                    for kind, di in (("A", 0), ("C", 0), ("A", 1)):
                        for g in range(G):
                            if offset_of(kind, 2 * g) + OFFSETS * di - HR_LEAD == o:
                                hidden_fill(st, kind, di, g)
                    for what in TENSOR_FILLS.get(o, ()):
                        tensor_fill(st, what)
                    kind, q = kind_at(o)
                    if st.has(kind):
                        granule(st, kind, q)

            run_steps(pe, step, 3, 2)

            for kind in "ABC":
                pe.wait_ge(pooled_done[kind], BLOCKS)
            for k in range(4):
                dst = (hr_ps, sel_ps)[k // 2]
                for c in range(CHUNKS):
                    last = pe.matmul(dst[0:HALF, k % 2, c * P:(c + 1) * P], pooled[:, c, k * HALF:(k + 1) * HALF],
                                     ident[:, :], start=True, stop=True, is_transpose=True)
                last.then_inc(top_t, 1)
            pe.wait_ge(top_loaded, 7 * 16)
            pe.wait_ge(top_copied, 4)
            for m in range(4):
                dst = acc[m // 2][:, m % 2, :]
                for k in range(4):
                    pe.matmul(dst, w1t[:, k, m * P:(m + 1) * P], ht[:, k, :], start=(k == 0), stop=False)
                pe.matmul(dst, w1d[:, m * P:(m + 1) * P], denset, start=False, stop=True).then_inc(top_mm, 1)
            pe.wait_ge(top_act, 4)
            for m in range(2):
                for k in range(4):
                    last = pe.matmul(hr_ps[:, m, :], w2t[:, k, m * P:(m + 1) * P], h1[:, k, :], start=(k == 0),
                                     stop=(k == 3))
                last.then_inc(top_mm, 1)
            pe.wait_ge(top_act, 6)
            for k in range(2):
                last = pe.matmul(sel_ps[0:1, 0, :], w3t[:, k:k + 1], h2[:, k, :], start=(k == 0), stop=(k == 1))
            last.then_inc(top_mm, 1)


def selection():
    import numpy as np
    s = np.zeros((PARTS, J + 1 + T0, KT), np.float32)
    for part in range(3):
        for j in range(J):
            for p in range(KT):
                m = MG * j + p // NGRP
                if m < F:
                    s[F * part + m, j, p] = 1
        for p in range(K0):
            s[F * part + p % F, J, p] = 1
            for t in range(T0):
                shift = SPT * t + p // F
                if shift < SHIFTS:
                    s[F * part + (p % F + shift) % F, J + 1 + t, p] = 1
    s[PARTS - 1, J, K0] = 1
    s[PARTS - 1, J + 1, K0] = 1
    return s


def kernel(**inputs):
    import ml_dtypes
    import numpy as np
    import concourse.bacc as bacc
    from concourse import mybir
    from concourse.bass_utils import run_bass_kernel_spmd

    a = {k: np.ascontiguousarray(v) for k, v in inputs.items()}

    zero = np.zeros((1, UNITS), np.float32)
    rows0 = np.concatenate([a["L0_rec_W0"], a["L0_rec_b0"][None], zero])
    bias_row, zero_row = F * F, F * F + 1
    direct = np.full((K0 + 1, T0), zero_row)
    swapped = np.full((K0 + 1, T0), zero_row)
    for t in range(T0):
        for p in range(K0):
            s, m = SPT * t + p // F, p % F
            if s < SHIFTS:
                n = (m + s) % F
                direct[p, t] = m * F + n
                if s:
                    swapped[p, t] = n * F + m
    direct[K0, 0] = bias_row

    tiles = np.full((KT + 1, G * J), F * HALF + 1)
    for g in range(G):
        for j in range(J):
            for p in range(KT):
                m, n = MG * j + p // NGRP, NGRP * g + p % NGRP
                if m < F:
                    tiles[p, J * g + j] = m * HALF + n
    tiles[KT, 0] = F * HALF

    def packed(layer):
        rows = np.concatenate([a[f"L0_rec_W{layer}"], a[f"L0_rec_b{layer}"][None], zero])
        return rows[tiles]

    arrays = {
        "ids": np.ascontiguousarray(a["ids"].reshape(CHUNKS, P, F).transpose(1, 0, 2)),
        "w0_direct": rows0[direct], "w0_swapped": rows0[swapped],
        "w1": packed(1), "w2": packed(2),
        "sel": selection().astype(ml_dtypes.bfloat16),
        "identity": np.eye(P, dtype=np.float32),
        "w_top1": np.ascontiguousarray(a["W_top1"][:4 * HALF].reshape(4, HALF, 512).transpose(1, 0, 2)),
        "w_top1_dense": a["W_top1"][4 * HALF:],
        "b_top1": np.ascontiguousarray(a["b_top1"].reshape(4, P).T),
        "w_top2": np.ascontiguousarray(a["W_top2"].reshape(4, P, 256).transpose(1, 0, 2)),
        "b_top2": np.ascontiguousarray(a["b_top2"].reshape(2, P).T),
        "w_top3": np.ascontiguousarray(a["W_top3"].reshape(2, P).T),
        "dense_t": np.ascontiguousarray(a["dense_ctx"].T),
    }
    for f in range(F):
        arrays[f"tbl_{f}"] = a[f"tbl_{f}"]

    nc = bacc.Bacc("TRN2", target_bir_lowering=False, num_devices=1)
    dram = {name: nc.dram_tensor(name, v.shape, mybir.dt.from_np(v.dtype), kind="ExternalInput").ap()
            for name, v in arrays.items()}
    out = nc.dram_tensor("y", (B, 1), mybir.dt.float32, kind="ExternalOutput").ap()
    build(nc, dram["ids"], [dram[f"tbl_{f}"] for f in range(F)], dram["w0_direct"], dram["w0_swapped"], dram["w1"],
          dram["w2"], dram["sel"], dram["identity"], dram["w_top1"], dram["w_top1_dense"], dram["b_top1"],
          dram["w_top2"], dram["b_top2"], dram["w_top3"], dram["dense_t"], out)
    result = run_bass_kernel_spmd(nc, [arrays], core_ids=[0])
    return result.results[0]["y"]
```

```python
B, F, D, DENSE = 512, 39, 32, 16
P = 128
UNITS, HALF = 200, 100
CHUNKS = B // P
DB = 2
COLS = DB * P
BLOCKS = CHUNKS * D // DB
MG, NGRP = 5, 25
KT = MG * NGRP
J = (F + MG - 1) // MG
G = HALF // NGRP
KLAST = (F - MG * (J - 1)) * NGRP
SHIFTS = (F + 1) // 2
SPT = 3
K0 = SPT * F
T0 = (SHIFTS + SPT - 1) // SPT
K0LAST = (SHIFTS - SPT * (T0 - 1)) * F
PARTS = 3 * F + 1
TG = 4
QA = J * G // TG
QB = (T0 + TG - 1) // TG
OFFSETS = 2 * QA + QB
TILES = T0 + 2 * J * G
ZF_SLOTS, ZH_SLOTS, ZL_SLOTS = 3, 4, 3
SUB_D = 8
SUB_BLOCKS = SUB_D // DB
SUBS = D // SUB_D
SPLIT_OPS = 5

SUM_AT = {"A": 13, "B": 15, "C": 5}
COPY_SMALL_AT = {"A": 11, "B": 13, "C": 4}
HE_AT = {("A", 0): 15, ("A", 1): 15, ("C", 0): 3, ("C", 1): 9}
ZL_LAG = 3
GATHER_AT, SPLIT_AT = (9, 10, 11, 12), (3, 4, 10, 11, 12)
SPLIT_STEP = -(-F // len(GATHER_AT))
XT_COPY_AT, A3_COPY_AT, XB_COPY_AT = 19, 19, 11
HR_AT = {("A", 0): 13, ("A", 1): 15, ("C", 0): 4, ("C", 1): 6}
FILLS = ((15, 'T', 1), (17, 'A3', 1), (0, 0, 0), (1, 1, 0), (5, 2, 0), (5, 3, 0), (7, 'X0', 0), (8, 'X1', 0), (10, 'X2', 0), (11, 'X3', 0))
POOL_LOW = {2, 3, 4, 5, 6, 10, 12, 13, 14, 17}


def offset_of(kind, q):
    return {"A": 0, "B": QA, "C": QA + QB}[kind] + q


def kind_at(o):
    if o < QA:
        return "A", o
    if o < QA + QB:
        return "B", o - QA
    return "C", o - QA - QB


def exists(kind, i):
    return {"A": 0 <= i <= BLOCKS - 1, "B": -1 <= i <= BLOCKS - 2, "C": 1 <= i <= BLOCKS}[kind]


def build_counts():
    z, low_pool, low_dve, hr, order = {}, {}, {}, {}, []
    for i in range(-1, BLOCKS + 1):
        for o in range(OFFSETS):
            kind, q = kind_at(o)
            if not exists(kind, i):
                continue
            z[kind, i, q] = len(z) + 1
            if o in POOL_LOW:
                low_pool[kind, i, q] = len(low_pool) + 1
            else:
                low_dve[kind, i, q] = len(low_dve) + 1
            if kind != "B" and q % 2 == 0:
                hr[kind, i, q // 2] = len(hr) + 1
                order.append((kind, i, q // 2))
    return z, low_pool, low_dve, hr, order


def build(nc, ids, tables, w0_direct, w0_swapped, w1, w2, sel_in, identity_in, w_top1, w_top1_dense,
          b_top1, w_top2, b_top2, w_top3, dense_t, out):
    import concourse.bass as bass
    from concourse import mybir
    from contextlib import ExitStack

    f32, f32r = mybir.dt.float32, mybir.dt.float32r
    bf16, i32 = mybir.dt.bfloat16, mybir.dt.int32
    ALU, ACT = mybir.AluOpType, mybir.ActivationFunctionType

    Z, LOWP, LOWD, HRN, HR_ORDER = build_counts()
    N_GRANULES = len(Z)
    POOL_SET = set(LOWP)

    class Step:

        def __init__(self, rep, expr=None):
            self.rep, self.expr = rep, expr

        def has(self, kind, di=0):
            return exists(kind, self.rep + di)

        def count(self, f):
            if self.expr is None:
                return f(self.rep)
            slope = (f(self.rep + 6) - f(self.rep)) // 6
            return self.expr * slope + (f(self.rep) - slope * self.rep)

    def run_steps(engine, step, first, unroll, begin=-2, last=BLOCKS + 1):
        for i in range(begin, first):
            step(Step(i))
        end = BLOCKS - 2
        assert (end - first) % unroll == 0
        with engine.Fori(0, (end - first) // unroll) as turn:
            for k in range(unroll):
                step(Step(first + k, turn * unroll + (first + k)))
        for i in range(end, last + 1):
            step(Step(i))

    with ExitStack() as ctx:
        def sb(name, shape, dt=f32):
            return ctx.enter_context(nc.sbuf_tensor(name, shape, dt))

        def sem(name):
            return ctx.enter_context(nc.semaphore(name))

        weights = sb("weights", [P, TILES, 2 * UNITS], f32r)
        xb = sb("x_repeated", [P, 3, J, COLS])
        zf = sb("z_full", [P, ZF_SLOTS, TG, COLS])
        zh = sb("z_high", [P, ZH_SLOTS, TG, COLS], f32r)
        zl = sb("z_low", [P, ZL_SLOTS, TG, COLS], f32r)
        a3 = sb("x_three_times", [P, COLS])
        sel = sb("selection", [P, J + 1 + T0, KT], bf16)
        xt3 = sb("x_parts_transposed", [P, COLS], bf16)
        px = sb("x_parts", [P, 2, DB * PARTS], bf16)
        sum_a = sb("sum_a", [P, 2, DB, UNITS])
        sum_bc = sb("sum_bc", [P, DB, UNITS])
        he = sb("hidden_repeated", [P, 2, DB, KT])
        pooled = sb("pooled", [P, CHUNKS, 2 * UNITS])
        ident = sb("ident", [P, P])
        identb = sb("identb", [P, P], bf16)
        xg = sb("x_gathered", [P, F, D])
        p3 = sb("x_split", [P, SUB_BLOCKS, DB * PARTS], bf16)
        one = sb("one", [P, 1])
        idx = sb("idx", [P, F], i32)
        parts_dram = nc.dram_tensor("x_parts_dram", [BLOCKS, P, DB * PARTS], bf16, kind="Internal").ap()

        acc = [ctx.enter_context(nc.psum_tensor(f"acc{s}", [P, DB, 512], f32)) for s in range(2)]
        hr_ps = ctx.enter_context(nc.psum_tensor("hr_ps", [P, 2, 512], f32))
        sel_ps = ctx.enter_context(nc.psum_tensor("sel_ps", [P, 2, 512], f32))

        xb_flat = xb[:, :, :, :].rearrange("p a j c -> p (a j c)")
        zf_flat = zf[:, :, :, :].rearrange("p a j c -> p (a j c)")
        GW = J * UNITS
        stage = [xb_flat[:, s * GW:(s + 1) * GW].rearrange("p (t o) -> p t o", o=UNITS) for s in range(3)]
        stage.append(zf_flat[:, 0:GW].rearrange("p (t o) -> p t o", o=UNITS))

        w1t = xb_flat[0:HALF, 0:4 * 512].rearrange("p (k n) -> p k n", k=4)
        w2t = xb_flat[:, 2048:3072].rearrange("p (k n) -> p k n", k=4)
        w3t = xb_flat[:, 3072:3074]
        b1t = xb_flat[:, 3074:3078]
        b2t = xb_flat[:, 3078:3080]
        ht = xb_flat[0:HALF, 3080:5128].rearrange("p (k n) -> p k n", k=4)
        h2 = xb_flat[:, 3080:4104].rearrange("p (k n) -> p k n", k=2)
        h1 = zf_flat[:, 0:2048].rearrange("p (k n) -> p k n", k=4)
        denset = zf_flat[0:DENSE, 2048:2560]
        w1d = zf_flat[0:DENSE, 2560:3072]
        y_row = xb_flat[0:1, 5200:5712]

        const_loaded = sem("const_loaded")
        ids_loaded = sem("ids_loaded")
        ids_next = sem("ids_next")
        stage_loaded = [sem(f"stage_loaded{s}") for s in range(4)]
        w_added = sem("w_added")
        w_high = sem("w_high")
        w_low = sem("w_low")
        identb_ready = sem("identb_ready")
        filled = sem("filled")
        pooled_zero = sem("pooled_zero")
        gathered = sem("gathered")
        split_step = sem("split_step")
        parts_stored = sem("parts_stored")
        px_loaded = [sem(f"px_loaded{s}") for s in range(2)]
        sel_done = sem("sel_done")
        sel_copied = sem("sel_copied")
        bt_half = sem("bt_half")
        he_done = sem("he_done")
        hr_done = sem("hr_done")
        z_done = sem("z_done")
        zh_done = sem("zh_done")
        low_pool = sem("low_pool")
        low_dve = sem("low_dve")
        pe_used = sem("pe_used")
        lo_copied = {k: sem(f"lo_copied_{k}") for k in "ABC"}
        sum_done = {k: sem(f"sum_done_{k}") for k in "ABC"}
        pooled_step = sem("pooled_step")
        pooled_done = {k: sem(f"pooled_done_{k}") for k in "ABC"}
        top_loaded = sem("top_loaded")
        top_t = sem("top_t")
        top_copied = sem("top_copied")
        top_mm = sem("top_mm")
        top_act = sem("top_act")
        out_stored = sem("out_stored")

        ended = {"A": lambda i: i + 1, "B": lambda i: i + 2, "C": lambda i: i}

        def phase_set(kind, i):
            return (3 * i + {"A": 1, "B": 2, "C": 3}[kind]) % 2

        def tiles_of(kind, q):
            if kind == "B":
                return [(t - TG * q, t, K0 + 1 if t == 0 else (K0LAST if t == T0 - 1 else K0),
                         K0LAST if t == T0 - 1 else K0) for t in range(TG * q, min(T0, TG * q + TG))]
            base = T0 + (J * G if kind == "C" else 0)
            rows = []
            for u in range(TG):
                j = TG * (q % 2) + u
                k = KLAST if j == J - 1 else KT
                rows.append((u, base + J * (q // 2) + j, KT + 1 if (q, j) == (0, 0) else k, k))
            return rows

        def before(kind, di, q):
            o = offset_of(kind, q) + OFFSETS * di - ZL_LAG
            k, r = kind_at(o % OFFSETS)
            return k, o // OFFSETS, r

        block = ctx.enter_context(nc.Block())

        @block.sync
        def _(sp):
            sp.dma_start(idx[:, :], ids[:, 0, :]).then_inc(ids_loaded, 16)
            sp.dma_start(stage[0][0:K0 + 1, 0:T0, :], w0_direct).then_inc(stage_loaded[0], 16)
            sp.dma_start(stage[1][0:K0 + 1, 0:T0, :], w0_swapped).then_inc(stage_loaded[1], 16)
            sp.dma_start(sel[0:PARTS, :, :], sel_in).then_inc(const_loaded, 16)
            sp.dma_start(ident[:, :], identity_in).then_inc(const_loaded, 16)
            for n in range(2 * G):
                s = (n + 2) % 4
                if n >= 2:
                    sp.wait_ge(w_high, max(1, n - 2))
                    sp.wait_ge(w_low, max(1, n - 2))
                src = (w1, w2)[n // G]
                g = n % G
                sp.dma_start(stage[s][0:KT + 1, 0:J, :], src[:, J * g:J * (g + 1), :]).then_inc(stage_loaded[s], 16)

            def load_parts(i, k):
                sp.dma_start(px[:, k % 2, :], parts_dram[bass.ds(i, 1), :, :].rearrange("k b n -> b (k n)")
                             ).then_inc(px_loaded[k % 2], 16)

            for k in range(4):
                if k == 0:
                    sp.wait_ge(parts_stored, 16)
                if k >= 2:
                    sp.wait_ge(sel_done, 10 * (k - 2) + 1)
                load_parts(k, k)
            with sp.Fori(1, BLOCKS // 4) as turn:
                sp.wait_ge(parts_stored, turn * 16 + 16)
                for k in range(4):
                    sp.wait_ge(sel_done, turn * 40 + (10 * (k - 2) + 1))
                    load_parts(turn * 4 + k, k)

            sp.wait_ge(z_done, N_GRANULES)
            sp.wait_ge(zh_done, N_GRANULES)
            sp.wait_ge(low_pool, len(LOWP))
            sp.wait_ge(low_dve, len(LOWD))
            for dst, src in ((w1t, w_top1), (w1d, w_top1_dense), (denset, dense_t), (b1t, b_top1), (w2t, w_top2),
                             (b2t, b_top2), (w3t, w_top3)):
                sp.dma_start(dst, src).then_inc(top_loaded, 16)
            sp.wait_ge(top_act, 7)
            sp.dma_start(out.rearrange("b o -> o b"), y_row).then_inc(out_stored, 16)
            sp.wait_ge(out_stored, 16)

        @block.gpsimd
        def _(pool):
            def gather(f):
                pool.indirect_dma_start(xg[:, f, :], None, tables[f],
                                        bass.IndirectOffsetOnAxis(idx[:, f:f + 1], 0)).then_inc(gathered, 16)

            one_b = one[:, :].unsqueeze(2).to_broadcast([P, F, SUB_D])
            x_now = lambda s: xg[:, :, SUB_D * s:SUB_D * (s + 1)]
            parts = p3[:, :, :].rearrange("p k (e n) -> p (k e) n", e=DB)
            part_of = lambda part: parts[:, :, F * part:F * (part + 1)].rearrange("p d f -> p f d")

            def split_op(c, s, k):
                n = c * SUBS + s
                if k == SPLIT_OPS:
                    pool.wait_ge(split_step, n * SPLIT_OPS + SPLIT_OPS + 1)
                    pool.dma_start(parts_dram[bass.ds(n * SUB_BLOCKS, SUB_BLOCKS), :, :].rearrange("k b n -> b k n"),
                                   p3[:, :, :]).then_inc(parts_stored, 16)
                    return
                pool.wait_ge(split_step, n * SPLIT_OPS + k + 1)
                if k == 0 and not (isinstance(n, int) and n == 0):
                    pool.wait_ge(parts_stored, n * 16)
                if k % 2 == 0:
                    pool.tensor_tensor(part_of(k // 2), x_now(s), one_b, ALU.mult).then_inc(split_step, 1)
                else:
                    pool.tensor_tensor(x_now(s), x_now(s), part_of(k // 2), ALU.subtract).then_inc(split_step, 1)

            pool.wait_ge(ids_loaded, 16)
            for f in range(F):
                gather(f)
            pool.memset(one[:, :], 1.0)
            pool.memset(p3[:, :, :], 1.0).then_inc(split_step, 1)
            pool.wait_ge(gathered, 16 * F)
            for s in range(SUBS):
                for k in range(SPLIT_OPS + 1):
                    split_op(0, s, k)

            def low_part(st, kind, di, q):
                z = lambda i: Z[kind, i + di, q]
                slot_of = Z[kind, st.rep + di, q] - 1
                pool.wait_ge(zh_done, st.count(z))
                if Z[kind, st.rep + di, q] > ZL_SLOTS:
                    pool.wait_ge(pe_used, st.count(lambda i: z(i) - ZL_SLOTS))
                n = len(tiles_of(kind, q))
                pool.tensor_tensor(zl[0:KT, slot_of % ZL_SLOTS, 0:n, :], zf[0:KT, slot_of % ZF_SLOTS, 0:n, :],
                                   zh[0:KT, slot_of % ZH_SLOTS, 0:n, :].bitcast(f32),
                                   ALU.subtract).then_inc(low_pool, 1)

            def fetch(c, k, o):
                if k == 0 and o == 0:
                    pool.wait_ge(gathered, c * (16 * F))
                    pool.wait_ge(split_step, c * (SUBS * SPLIT_OPS) + 1)
                    pool.dma_start(idx[:, :], ids[:, bass.ds(c, 1), :].rearrange("p c f -> p (c f)")
                                   ).then_inc(ids_next, 16)
                if k < SPLIT_STEP:
                    f = k * len(GATHER_AT) + GATHER_AT.index(o) if o in GATHER_AT else F
                    if f < F:
                        gather(f)
                elif k < SPLIT_STEP + SUBS and o in SPLIT_AT:
                    if k == SPLIT_STEP and o == SPLIT_AT[0]:
                        pool.wait_ge(gathered, c * (16 * F) + 16 * F)
                    split_op(c, k - SPLIT_STEP, SPLIT_AT.index(o))
                    if o == SPLIT_AT[-1]:
                        split_op(c, k - SPLIT_STEP, SPLIT_OPS)

            def step(st, c=None, k=None):
                for o in range(OFFSETS):
                    kind, q = kind_at(o)
                    lk, ldi, lq = before(kind, 0, q)
                    if k == 0 and o == GATHER_AT[0]:
                        pool.wait_ge(ids_next, c * 16)
                    if st.has(lk, ldi) and (lk, st.rep + ldi, lq) in POOL_SET:
                        low_part(st, lk, ldi, lq)
                    if c is not None:
                        fetch(c, k, o)

            first, per_chunk = 2, BLOCKS // CHUNKS
            for i in range(-2, first):
                step(Step(i))
            with pool.Fori(0, CHUNKS - 1) as turn:
                for k in range(per_chunk):
                    step(Step(first + k, turn * per_chunk + (first + k)), turn + 1, k)
            run_steps(pool, step, first + per_chunk * (CHUNKS - 1), 2, begin=first + per_chunk * (CHUNKS - 1))
            pool.wait_ge(parts_stored, 16 * CHUNKS * SUBS)

        @block.scalar
        def _(act):
            act.wait_ge(const_loaded, 32)
            act.activation(identb[:, :], ident[:, :], ACT.Copy).then_inc(identb_ready, 1)

            act.wait_ge(w_added, 1)
            act.activation(weights[0:K0 + 1, 0:T0, 0:UNITS], stage[0][0:K0 + 1, 0:T0, :], ACT.Copy).then_inc(w_high, 1)
            for n in range(2 * G):
                s = (n + 2) % 4
                act.wait_ge(stage_loaded[s], 16 * (1 + (n + 2) // 4))
                act.activation(weights[0:KT + 1, T0 + J * n:T0 + J * (n + 1), 0:UNITS], stage[s][0:KT + 1, :, :],
                               ACT.Copy).then_inc(w_high, 1)
            act.wait_ge(w_low, 1 + 2 * G)
            act.wait_ge(filled, 1)

            def high_part(st, kind, q):
                z = lambda i: Z[kind, i, q]
                n0 = Z[kind, st.rep, q]
                act.wait_ge(z_done, st.count(z))
                if n0 > ZH_SLOTS:
                    act.wait_ge(pe_used, st.count(lambda i: z(i) - ZH_SLOTS))
                n = len(tiles_of(kind, q))
                act.activation(zh[0:KT, (n0 - 1) % ZH_SLOTS, 0:n, :], zf[0:KT, (n0 - 1) % ZF_SLOTS, 0:n, :],
                               ACT.Copy).then_inc(zh_done, 1)

            def copy_small(st, kind, di):
                if not st.has(kind, di):
                    return
                i = st.rep + di
                act.wait_ge(pe_used, st.count(lambda i: Z[kind, i + di, (QB if kind == "B" else QA) - 1]))
                if kind == "A":
                    dst = sum_a[:, i % 2, :, :]
                    if i >= 2:
                        act.wait_ge(pooled_done["A"], st.count(lambda i: ended["A"](i + di - 2)))
                        act.wait_ge(he_done, st.count(lambda i: HRN["C", i + di - 1, G - 1]))
                elif kind == "B":
                    dst = sum_bc[:, :, :]
                    if i >= 2:
                        act.wait_ge(pooled_done["C"], st.count(lambda i: ended["C"](i + di - 1)))
                    elif i >= 0:
                        act.wait_ge(pooled_done["B"], ended["B"](i - 1))
                        act.wait_ge(he_done, HRN["A", i, G - 1])
                else:
                    dst = sum_bc[:, :, :]
                    act.wait_ge(pooled_done["B"], st.count(lambda i: min(ended["B"](i + di), BLOCKS)))
                    if exists("A", i + 1):
                        act.wait_ge(he_done, st.count(lambda i: HRN["A", i + di + 1, G - 1]))
                act.activation(dst, acc[phase_set(kind, i)][:, :, UNITS:2 * UNITS], ACT.Copy).then_inc(lo_copied[kind], 1)

            def repeat_hidden(st, kind, di, g):
                if not st.has(kind, di):
                    return
                i = st.rep + di
                n0 = HRN[kind, i, g]
                if kind == "A":
                    act.wait_ge(sum_done["B"], st.count(lambda i: ended["B"](i + di - 1)))
                    v = sum_bc[:, :, NGRP * g:NGRP * (g + 1)]
                else:
                    act.wait_ge(sum_done["A"], st.count(lambda i: ended["A"](i + di - 1)))
                    v = sum_a[:, (i - 1) % 2, :, NGRP * g:NGRP * (g + 1)]
                if n0 > 2:
                    act.wait_ge(hr_done, st.count(lambda i: HRN[kind, i + di, g] - 2))
                act.activation(he[:, g % 2, :, :].rearrange("p e (r n) -> p e r n", r=MG),
                               v.unsqueeze(2).to_broadcast([P, DB, MG, NGRP]), ACT.Relu).then_inc(he_done, 1)

            def copy_parts(st, di):
                if st.has("B", di):
                    act.wait_ge(sel_done, st.count(lambda i: 10 * (i + di + 1) + 1))
                    act.activation(xt3[0:PARTS, :], sel_ps[0:PARTS, 0, 0:COLS // 2].bitcast(bf16),
                                   ACT.Copy).then_inc(sel_copied, 1)

            def copy_a3(st, di):
                if st.has("B", di):
                    act.wait_ge(sel_done, st.count(lambda i: 10 * (i + di + 1) + 2))
                    if st.rep + di >= 0:
                        act.wait_ge(z_done, st.count(lambda i: Z["B", i + di - 1, QB - 1]))
                    act.activation(a3[0:KT, :], sel_ps[0:KT, 1, 0:COLS], ACT.Copy).then_inc(sel_copied, 1)

            def copy_xb(st, k):
                if st.has("B"):
                    b = st.rep + 1
                    act.wait_ge(sel_done, st.count(lambda i: 10 * (i + 1) + 7 + k))
                    if b >= 3:
                        act.wait_ge(z_done, st.count(lambda i: Z["C", i - 1, QA - 1]))
                    act.activation(xb[0:KT, b % 3, 2 * k:2 * k + 2, :].rearrange("p j c -> p (j c)"),
                                   sel_ps[0:KT, k % 2, :], ACT.Copy).then_inc(sel_copied, 1)

            def step(st):
                for o in range(OFFSETS):
                    if o == COPY_SMALL_AT["C"]:
                        copy_small(st, "C", -1)
                    if o == COPY_SMALL_AT["A"]:
                        copy_small(st, "A", 0)
                    if o == COPY_SMALL_AT["B"]:
                        copy_small(st, "B", 0)
                    if o == XT_COPY_AT % OFFSETS:
                        copy_parts(st, 1 - XT_COPY_AT // OFFSETS)
                    if o == A3_COPY_AT % OFFSETS:
                        copy_a3(st, 1 - A3_COPY_AT // OFFSETS)
                    if XB_COPY_AT <= o < XB_COPY_AT + 4:
                        copy_xb(st, o - XB_COPY_AT)
                    for g in range(G):
                        for kind in "CA":
                            at = HE_AT[kind, g // 2]
                            if o == at % OFFSETS:
                                repeat_hidden(st, kind, (kind == "A") - at // OFFSETS, g)
                    kind, q = kind_at(o)
                    if st.has(kind):
                        high_part(st, kind, q)

            run_steps(act, step, 2, 6)

            for k in range(4):
                act.wait_ge(top_t, k + 1)
                if k == 0:
                    act.wait_ge(z_done, N_GRANULES)
                src = (hr_ps, sel_ps)[k // 2][0:HALF, k % 2, :]
                act.activation(ht[:, k, :], src, ACT.Copy).then_inc(top_copied, 1)
            act.wait_ge(top_loaded, 7 * 16)
            act.wait_ge(low_pool, len(LOWP))
            act.wait_ge(low_dve, len(LOWD))
            for m in range(4):
                act.wait_ge(top_mm, m + 1)
                act.activation(h1[:, m, :], acc[m // 2][:, m % 2, :], ACT.Relu, bias=b1t[:, m:m + 1]).then_inc(top_act, 1)
            for m in range(2):
                act.wait_ge(top_mm, 5 + m)
                act.activation(h2[:, m, :], hr_ps[:, m, :], ACT.Relu, bias=b2t[:, m:m + 1]).then_inc(top_act, 1)
            act.wait_ge(top_mm, 7)
            act.activation(y_row, sel_ps[0:1, 0, :], ACT.Copy).then_inc(top_act, 1)

        @block.vector
        def _(dve):
            dve.memset(zh[:, :, :, :].bitcast(f32), 1.0).then_inc(filled, 1)
            dve.memset(pooled[:, :, :], 0.0).then_inc(pooled_zero, 1)
            dve.wait_ge(stage_loaded[0], 16)
            dve.wait_ge(stage_loaded[1], 16)
            s0, s1 = stage[0][0:K0 + 1, 0:T0, :], stage[1][0:K0 + 1, 0:T0, :]
            dve.tensor_tensor(s0, s0, s1, ALU.add).then_inc(w_added, 1)
            dve.wait_ge(w_high, 1)
            dve.tensor_tensor(weights[0:K0 + 1, 0:T0, UNITS:2 * UNITS], s0,
                              weights[0:K0 + 1, 0:T0, 0:UNITS].bitcast(f32), ALU.subtract).then_inc(w_low, 1)
            for n in range(2 * G):
                w = weights[0:KT + 1, T0 + J * n:T0 + J * (n + 1), :]
                dve.wait_ge(w_high, n + 2)
                dve.tensor_tensor(w[:, :, UNITS:2 * UNITS], stage[(n + 2) % 4][0:KT + 1, :, :],
                                  w[:, :, 0:UNITS].bitcast(f32), ALU.subtract).then_inc(w_low, 1)
            dve.wait_ge(pooled_zero, 1)
            pooled_steps = [0]

            def product(st, kind, q):
                z = lambda i: Z[kind, i, q]
                n0 = Z[kind, st.rep, q]
                slot = (n0 - 1) % ZF_SLOTS
                if n0 > ZF_SLOTS:
                    was = [key for key, value in Z.items() if value == n0 - ZF_SLOTS][0]
                    wk, wi, wq = was
                    di = wi - st.rep
                    if was in POOL_SET:
                        dve.wait_ge(low_pool, st.count(lambda i: LOWP[wk, i + di, wq]))
                    else:
                        dve.wait_ge(low_dve, st.count(lambda i: LOWD[wk, i + di, wq]))
                if kind == "B":
                    for h in range(2):
                        fill = 2 * q + h
                        n = min(2, T0 - 2 * fill)
                        dve.wait_ge(sel_done, st.count(lambda i: 10 * (i + 1) + 3 + fill))
                        if fill == 0:
                            dve.wait_ge(sel_copied, st.count(lambda i: 6 * (i + 1) + 2))
                        ins = dve.tensor_tensor(
                            zf[0:KT, slot, 2 * h:2 * h + n, :],
                            a3[0:KT, :].unsqueeze(1).to_broadcast([KT, n, COLS]),
                            sel_ps[0:KT, fill % 2, 0:n * COLS].rearrange("p (t c) -> p t c", t=n), ALU.mult)
                        ins.then_inc((bt_half, z_done)[h], 1)
                    return
                b = st.rep if kind == "A" else st.rep - 1
                if q == 0 and kind == "A":
                    dve.wait_ge(sel_copied, st.count(lambda i: 6 * i + 6))
                if q % 4 == 0:
                    dve.wait_ge(hr_done, st.count(lambda i: HRN[kind, i, q // 2 + 1]))
                j0 = TG * (q % 2)
                dve.tensor_tensor(zf[0:KT, slot, :, :], xb[0:KT, b % 3, j0:j0 + TG, :],
                                  hr_ps[0:KT, q // 4, (q // 2 % 2) * COLS:(q // 2 % 2 + 1) * COLS].unsqueeze(1).to_broadcast([KT, TG, COLS]),
                                  ALU.mult).then_inc(z_done, 1)

            def low_part(st, kind, di, q):
                z = lambda i: Z[kind, i + di, q]
                n0 = Z[kind, st.rep + di, q]
                dve.wait_ge(zh_done, st.count(z))
                if n0 > ZL_SLOTS:
                    dve.wait_ge(pe_used, st.count(lambda i: z(i) - ZL_SLOTS))
                n = len(tiles_of(kind, q))
                dve.tensor_tensor(zl[0:KT, (n0 - 1) % ZL_SLOTS, 0:n, :], zf[0:KT, (n0 - 1) % ZF_SLOTS, 0:n, :],
                                  zh[0:KT, (n0 - 1) % ZH_SLOTS, 0:n, :].bitcast(f32),
                                  ALU.subtract).then_inc(low_dve, 1)

            def add_and_pool(st, kind, di):
                if not st.has(kind, di):
                    return
                i = st.rep + di
                dst = sum_a[:, i % 2, :, :] if kind == "A" else sum_bc[:, :, :]
                dve.wait_ge(lo_copied[kind], st.count(lambda i: ended[kind](i + di)))
                dve.tensor_tensor(dst, acc[phase_set(kind, i)][:, :, 0:UNITS], dst, ALU.add).then_inc(sum_done[kind], 1)
                first = 0 if kind == "C" else HALF
                units = UNITS - first
                at = {"B": 0, "A": HALF, "C": 2 * HALF}[kind]
                db = {"A": 0, "B": 1, "C": -1}[kind] + di
                if st.expr is None:
                    c = (st.rep + db) // (BLOCKS // CHUNKS)
                    total = pooled[:, c, at:at + units]
                else:
                    c = (st.expr + db) // (BLOCKS // CHUNKS)
                    total = pooled[:, bass.ds(c, 1), at:at + units].rearrange("p c n -> p (c n)")
                dve.wait_ge(sum_done[kind], st.count(lambda i: ended[kind](i + di)))
                dve.scalar_tensor_tensor(total, dst[:, 0, first:UNITS], 0.0, total, ALU.max, ALU.add
                                         ).then_inc(pooled_step, 1)
                dve.wait_ge(pooled_step, st.count(lambda i: steps_before(i + di, kind) + 1))
                dve.scalar_tensor_tensor(total, dst[:, 1, first:UNITS], 0.0, total, ALU.max, ALU.add
                                         ).then_inc(pooled_done[kind], 1)

            def steps_before(i, kind):
                order = []
                for s in range(-1, BLOCKS + 2):
                    for k, di, o in (("C", -1, SUM_AT["C"]), ("A", 0, SUM_AT["A"]), ("B", 0, SUM_AT["B"])):
                        if exists(k, s + di):
                            order.append((k, s + di))
                return order.index((kind, i))

            def step(st):
                for o in range(OFFSETS):
                    if o == SUM_AT["C"]:
                        add_and_pool(st, "C", -1)
                    if o == SUM_AT["A"]:
                        add_and_pool(st, "A", 0)
                    if o == SUM_AT["B"]:
                        add_and_pool(st, "B", 0)
                    kind, q = kind_at(o)
                    lk, ldi, lq = before(kind, 0, q)
                    if st.has(lk, ldi) and (lk, st.rep + ldi, lq) not in POOL_SET:
                        low_part(st, lk, ldi, lq)
                    if st.has(kind):
                        product(st, kind, q)

            run_steps(dve, step, 2, 6)

        @block.tensor
        def _(pe):
            pe.wait_ge(identb_ready, 1)
            pe.wait_ge(w_low, 1 + 2 * G)

            def hidden_fill(st, kind, di, g):
                if not st.has(kind, di):
                    return
                n0 = HRN[kind, st.rep + di, g]
                pe.wait_ge(he_done, st.count(lambda i: HRN[kind, i + di, g]))
                if n0 > 4:
                    wk, wi, wg = HR_ORDER[n0 - 1 - g % 2 - 3]
                    wdi = wi - st.rep
                    pe.wait_ge(z_done, st.count(lambda i: Z[wk, i + wdi, 2 * wg + 1]))
                for e in range(DB):
                    last = pe.matmul(hr_ps[0:KT, g // 2, (g % 2) * COLS + e * P:(g % 2) * COLS + (e + 1) * P], he[:, g % 2, e, :], ident[:, :],
                                     start=True, stop=True, is_transpose=True)
                last.then_inc(hr_done, 1)

            def select(bank, half, which):
                return pe.matmul(sel_ps[0:KT, bank, half * COLS:(half + 1) * COLS], sel[0:PARTS, which, :],
                                 xt3[0:PARTS, :], start=True, stop=True)

            def tensor_fill(st, what, di):
                if not st.has("B", di):
                    return
                b = st.rep + di + 1
                if what == "T":
                    pe.wait_ge(px_loaded[b % 2], st.count(lambda i: 16 * ((i + di + 1) // 2 + 1)))
                    if b >= 1:
                        pe.wait_ge(sel_copied, st.count(lambda i: 6 * (i + di) + 5))
                    for e in range(DB):
                        last = pe.transpose(sel_ps[0:PARTS, 0, e * P // 2:(e + 1) * P // 2].bitcast(bf16),
                                            px[:, b % 2, e * PARTS:(e + 1) * PARTS], identb[:, :])
                    last.then_inc(sel_done, 1)
                    return
                if what == "A3":
                    pe.wait_ge(sel_copied, st.count(lambda i: 6 * (i + di + 1) + 1))
                    select(1, 0, J).then_inc(sel_done, 1)
                    return
                if what in (0, 1, 2, 3):
                    if what == 1:
                        pe.wait_ge(sel_copied, st.count(lambda i: 6 * (i + di + 1) + 2))
                    if what == 2:
                        pe.wait_ge(bt_half, st.count(lambda i: 2 * (i + di + 1) + 1))
                    if what == 3:
                        pe.wait_ge(z_done, st.count(lambda i: Z["B", i + di, 0]))
                    for h in range(min(2, T0 - 2 * what)):
                        last = select(what % 2, h, J + 1 + 2 * what + h)
                    last.then_inc(sel_done, 1)
                    return
                k = int(what[1])
                if k == 0:
                    pe.wait_ge(bt_half, st.count(lambda i: 2 * (i + di + 1) + 2))
                elif k == 1:
                    pe.wait_ge(z_done, st.count(lambda i: Z["B", i + di, 1]))
                else:
                    pe.wait_ge(sel_copied, st.count(lambda i: 6 * (i + di + 1) + 1 + k))
                for h in range(2):
                    last = select(k % 2, h, 2 * k + h)
                last.then_inc(sel_done, 1)

            def granule(st, kind, q):
                i = st.rep
                if q == 0:
                    if kind == "A":
                        pe.wait_ge(sum_done["B"], st.count(lambda i: ended["B"](i - 1)))
                    elif kind == "B" and i >= 2:
                        pe.wait_ge(sum_done["C"], st.count(lambda i: ended["C"](i - 1)))
                    elif kind == "B" and i == 1:
                        pe.wait_ge(sum_done["A"], 1)
                    elif kind == "C" and i < BLOCKS:
                        pe.wait_ge(sum_done["A"], st.count(ended["A"]))
                    elif kind == "C":
                        pe.wait_ge(sum_done["C"], BLOCKS - 2)
                z = lambda i: Z[kind, i, q]
                n0 = Z[kind, i, q] - 1
                key = (kind, i, q)
                pe.wait_ge(zh_done, st.count(z))
                if key in POOL_SET:
                    pe.wait_ge(low_pool, st.count(lambda i: LOWP[kind, i, q]))
                else:
                    pe.wait_ge(low_dve, st.count(lambda i: LOWD[kind, i, q]))
                phase = acc[phase_set(kind, i)]
                last_q = q == (QB if kind == "B" else QA) - 1
                tiles = tiles_of(kind, q)
                for e in range(DB):
                    for u, w, k_high, k_low in tiles:
                        high = zh[0:k_high, n0 % ZH_SLOTS, u, e * P:(e + 1) * P]
                        low = zl[0:k_low, n0 % ZL_SLOTS, u, e * P:(e + 1) * P]
                        pe.matmul(phase[:, e, 0:2 * UNITS], high, weights[0:k_high, w, :],
                                  start=(q == 0 and u == 0), stop=False)
                        last = pe.matmul(phase[:, e, UNITS:2 * UNITS], low, weights[0:k_low, w, 0:UNITS],
                                         start=False, stop=(last_q and u == len(tiles) - 1))
                last.then_inc(pe_used, 1)

            def step(st):
                for o in range(OFFSETS):
                    for g in range(G):
                        for kind in "CA":
                            at = HR_AT[kind, g // 2]
                            if o == at % OFFSETS:
                                hidden_fill(st, kind, (kind == "A") - at // OFFSETS, g)
                    for at, what, di in FILLS:
                        if at == o:
                            tensor_fill(st, what, di)
                    kind, q = kind_at(o)
                    if st.has(kind):
                        granule(st, kind, q)

            run_steps(pe, step, 2, 2)

            for kind in "ABC":
                pe.wait_ge(pooled_done[kind], BLOCKS)
            for k in range(4):
                dst = (hr_ps, sel_ps)[k // 2]
                for c in range(CHUNKS):
                    last = pe.matmul(dst[0:HALF, k % 2, c * P:(c + 1) * P], pooled[:, c, k * HALF:(k + 1) * HALF],
                                     ident[:, :], start=True, stop=True, is_transpose=True)
                last.then_inc(top_t, 1)
            pe.wait_ge(top_loaded, 7 * 16)
            pe.wait_ge(top_copied, 4)
            for m in range(4):
                dst = acc[m // 2][:, m % 2, :]
                for k in range(4):
                    pe.matmul(dst, w1t[:, k, m * P:(m + 1) * P], ht[:, k, :], start=(k == 0), stop=False)
                pe.matmul(dst, w1d[:, m * P:(m + 1) * P], denset, start=False, stop=True).then_inc(top_mm, 1)
            pe.wait_ge(top_act, 4)
            for m in range(2):
                for k in range(4):
                    last = pe.matmul(hr_ps[:, m, :], w2t[:, k, m * P:(m + 1) * P], h1[:, k, :], start=(k == 0),
                                     stop=(k == 3))
                last.then_inc(top_mm, 1)
            pe.wait_ge(top_act, 6)
            for k in range(2):
                last = pe.matmul(sel_ps[0:1, 0, :], w3t[:, k:k + 1], h2[:, k, :], start=(k == 0), stop=(k == 1))
            last.then_inc(top_mm, 1)


def selection():
    import numpy as np
    s = np.zeros((PARTS, J + 1 + T0, KT), np.float32)
    for part in range(3):
        for j in range(J):
            for p in range(KT):
                m = MG * j + p // NGRP
                if m < F:
                    s[F * part + m, j, p] = 1
        for p in range(K0):
            s[F * part + p % F, J, p] = 1
            for t in range(T0):
                shift = SPT * t + p // F
                if shift < SHIFTS:
                    s[F * part + (p % F + shift) % F, J + 1 + t, p] = 1
    s[PARTS - 1, J, K0] = 1
    s[PARTS - 1, J + 1, K0] = 1
    return s


def kernel(**inputs):
    import ml_dtypes
    import numpy as np
    import concourse.bacc as bacc
    from concourse import mybir
    from concourse.bass_utils import run_bass_kernel_spmd

    a = {k: np.ascontiguousarray(v) for k, v in inputs.items()}

    zero = np.zeros((1, UNITS), np.float32)
    rows0 = np.concatenate([a["L0_rec_W0"], a["L0_rec_b0"][None], zero])
    bias_row, zero_row = F * F, F * F + 1
    direct = np.full((K0 + 1, T0), zero_row)
    swapped = np.full((K0 + 1, T0), zero_row)
    for t in range(T0):
        for p in range(K0):
            s, m = SPT * t + p // F, p % F
            if s < SHIFTS:
                n = (m + s) % F
                direct[p, t] = m * F + n
                if s:
                    swapped[p, t] = n * F + m
    direct[K0, 0] = bias_row

    tiles = np.full((KT + 1, G * J), F * HALF + 1)
    for g in range(G):
        for j in range(J):
            for p in range(KT):
                m, n = MG * j + p // NGRP, NGRP * g + p % NGRP
                if m < F:
                    tiles[p, J * g + j] = m * HALF + n
    tiles[KT, 0] = F * HALF

    def packed(layer):
        rows = np.concatenate([a[f"L0_rec_W{layer}"], a[f"L0_rec_b{layer}"][None], zero])
        return rows[tiles]

    arrays = {
        "ids": np.ascontiguousarray(a["ids"].reshape(CHUNKS, P, F).transpose(1, 0, 2)),
        "w0_direct": rows0[direct], "w0_swapped": rows0[swapped],
        "w1": packed(1), "w2": packed(2),
        "sel": selection().astype(ml_dtypes.bfloat16),
        "identity": np.eye(P, dtype=np.float32),
        "w_top1": np.ascontiguousarray(a["W_top1"][:4 * HALF].reshape(4, HALF, 512).transpose(1, 0, 2)),
        "w_top1_dense": a["W_top1"][4 * HALF:],
        "b_top1": np.ascontiguousarray(a["b_top1"].reshape(4, P).T),
        "w_top2": np.ascontiguousarray(a["W_top2"].reshape(4, P, 256).transpose(1, 0, 2)),
        "b_top2": np.ascontiguousarray(a["b_top2"].reshape(2, P).T),
        "w_top3": np.ascontiguousarray(a["W_top3"].reshape(2, P).T),
        "dense_t": np.ascontiguousarray(a["dense_ctx"].T),
    }
    for f in range(F):
        arrays[f"tbl_{f}"] = a[f"tbl_{f}"]

    nc = bacc.Bacc("TRN2", target_bir_lowering=False, num_devices=1)
    dram = {name: nc.dram_tensor(name, v.shape, mybir.dt.from_np(v.dtype), kind="ExternalInput").ap()
            for name, v in arrays.items()}
    out = nc.dram_tensor("y", (B, 1), mybir.dt.float32, kind="ExternalOutput").ap()
    build(nc, dram["ids"], [dram[f"tbl_{f}"] for f in range(F)], dram["w0_direct"], dram["w0_swapped"], dram["w1"],
          dram["w2"], dram["sel"], dram["identity"], dram["w_top1"], dram["w_top1_dense"], dram["b_top1"],
          dram["w_top2"], dram["b_top2"], dram["w_top3"], dram["dense_t"], out)
    result = run_bass_kernel_spmd(nc, [arrays], core_ids=[0])
    return result.results[0]["y"]
```

```python
B, F, D, DENSE = 512, 39, 32, 16
P = 128
UNITS, HALF = 200, 100
CHUNKS = B // P
DB = 2
COLS = DB * P
BLOCKS = CHUNKS * D // DB
MG, NGRP = 5, 25
KT = MG * NGRP
J = (F + MG - 1) // MG
G = HALF // NGRP
KLAST = (F - MG * (J - 1)) * NGRP
SHIFTS = (F + 1) // 2
SPT = 3
K0 = SPT * F
T0 = (SHIFTS + SPT - 1) // SPT
K0LAST = (SHIFTS - SPT * (T0 - 1)) * F
PARTS = 3 * F + 1
TG = 4
QA = J * G // TG
QB = (T0 + TG - 1) // TG
OFFSETS = 2 * QA + QB
KTOP = HALF + DENSE // 4
TILES = T0 + 2 * J * G
ZF_SLOTS, ZH_SLOTS, ZL_SLOTS = 3, 4, 3
HR_SLOTS = 3
SUB_D = 8
SUB_BLOCKS = SUB_D // DB
SUBS = D // SUB_D
SPLIT_OPS = 5

SUM_AT = {"A": 15, "B": 7, "C": 5}
COPY_SMALL_AT = {"A": 13, "B": 6, "C": 4}
C_LATER = {BLOCKS - 1: 1, BLOCKS: QA + 1}
ZL_LAG = 3
GATHER_AT, SPLIT_AT = (2, 3, 4, 5), (3, 4, 6, 10, 12)
SPLIT_STEP = -(-F // len(GATHER_AT))
XT_COPY_AT, A3_COPY_AT = 11, 13
HIDDEN_COPY_AT = {"A": 17, "B": 10}
HIDDEN_AT = {"A": 13, "B": 5}
FILLS = ((7, 'T', 1), (9, 'A3', 1), (11, 0, 1), (12, 1, 1), (15, 2, 1), (15, 3, 1))
POOL_LOW = {2, 4, 5, 6, 8, 10, 12, 13, 14, 17}


def offset_of(kind, q):
    return {"B": 0, "A": QB, "C": QA + QB}[kind] + q


def kind_at(o):
    if o < QB:
        return "B", o
    if o < QA + QB:
        return "A", o - QB
    return "C", o - QA - QB


def exists(kind, i):
    return {"A": 0 <= i <= BLOCKS - 1, "B": -1 <= i <= BLOCKS - 2, "C": 1 <= i <= BLOCKS}[kind]


def build_counts():
    z, low_pool, low_dve, hidden, pair = {}, {}, {}, {}, {}
    for i in range(-1, BLOCKS + 1):
        for o in range(OFFSETS):
            kind, q = kind_at(o)
            if not exists(kind, i):
                continue
            z[kind, i, q] = len(z) + 1
            if o in POOL_LOW:
                low_pool[kind, i, q] = len(low_pool) + 1
            else:
                low_dve[kind, i, q] = len(low_dve) + 1
            if kind != "C" and q == 0:
                hidden[kind, i] = len(hidden) + 1
            if kind != "B" and q % 4 == 0:
                pair[kind, i, q // 4] = len(pair)
    return z, low_pool, low_dve, hidden, pair


def build(nc, ids, tables, w0_direct, w0_swapped, w1, w2, sel_in, identity_in, w_top1, 
          b_top1, w_top2, b_top2, w_top3, dense_t, out):
    import concourse.bass as bass
    from concourse import mybir
    from contextlib import ExitStack

    f32, f32r = mybir.dt.float32, mybir.dt.float32r
    bf16, i32 = mybir.dt.bfloat16, mybir.dt.int32
    ALU, ACT = mybir.AluOpType, mybir.ActivationFunctionType

    Z, LOWP, LOWD, HIDDEN, PAIR = build_counts()
    N_GRANULES = len(Z)
    POOL_SET = set(LOWP)
    PAIR_KEYS = list(PAIR)

    shifts = []

    class Step:

        def __init__(self, rep, expr=None, fused=False):
            self.rep, self.expr, self.fused = rep, expr, fused

        def has(self, kind, di=0):
            return exists(kind, self.rep + di)

        def count(self, f):
            if self.expr is None:
                return f(self.rep)
            slope = (f(self.rep + 6) - f(self.rep)) // 6
            const = f(self.rep) - slope * self.rep
            if self.fused:
                shifts.append(BLOCKS + len(shifts))
                return (self.expr + shifts[-1]) * slope + (const - slope * shifts[-1])
            return self.expr * slope + const

    def run_steps(engine, step, first, unroll, begin=-2, end=BLOCKS - 2, last=BLOCKS + 1):
        for i in range(begin, first):
            step(Step(i))
        assert (end - first) % unroll == 0
        with engine.Fori(0, (end - first) // unroll) as turn:
            for k in range(unroll):
                step(Step(first + k, turn * unroll + (first + k), engine is nc.sync))
        for i in range(end, last + 1):
            step(Step(i))

    with ExitStack() as ctx:
        def sb(name, shape, dt=f32):
            return ctx.enter_context(nc.sbuf_tensor(name, shape, dt))

        def sem(name):
            return ctx.enter_context(nc.semaphore(name))

        weights = sb("weights", [P, TILES, 2 * UNITS], f32r)
        xb = sb("x_repeated", [P, 3, J, COLS])
        zf = sb("z_full", [P, ZF_SLOTS, TG, COLS])
        zh = sb("z_high", [P, ZH_SLOTS, TG, COLS], f32r)
        zl = sb("z_low", [P, ZL_SLOTS, TG, COLS], f32r)
        a3 = sb("x_three_times", [P, COLS])
        sel = sb("selection", [P, 1 + T0, KT], bf16)
        xt3 = sb("x_parts_transposed", [P, COLS], bf16)
        px = sb("x_parts", [P, 2, DB * PARTS], bf16)
        sum_a = sb("sum_a", [P, DB, UNITS])
        sum_bc = sb("sum_bc", [P, DB, UNITS])
        hidden_t = sb("hidden_transposed", [P, COLS])
        hr = sb("hidden_repeated", [P, HR_SLOTS, 2, COLS])
        pooled = sb("pooled", [P, CHUNKS, 2 * UNITS])
        ident = sb("ident", [P, P])
        identb = sb("identb", [P, P], bf16)
        xg = sb("x_gathered", [P, F, D])
        p3 = sb("x_split", [P, SUB_BLOCKS, DB * PARTS], bf16)
        one = sb("one", [P, 1])
        idx = sb("idx", [P, F], i32)
        parts_dram = nc.dram_tensor("x_parts_dram", [BLOCKS, P, DB * PARTS], bf16, kind="Internal").ap()

        xt_dram = nc.dram_tensor("x_transposed_dram", [BLOCKS, MG * J, COLS], f32, kind="Internal").ap()

        hidden_dram = {k: nc.dram_tensor(f"hidden_dram_{k}", [BLOCKS, HALF, COLS], f32, kind="Internal").ap()
                       for k in "AB"}

        acc = [ctx.enter_context(nc.psum_tensor(f"acc{s}", [P, DB, 512], f32)) for s in range(2)]
        hr_ps = ctx.enter_context(nc.psum_tensor("hr_ps", [P, 2, 512], f32))
        sel_ps = ctx.enter_context(nc.psum_tensor("sel_ps", [P, 2, 512], f32))

        xb_flat = xb[:, :, :, :].rearrange("p a j c -> p (a j c)")
        zf_flat = zf[:, :, :, :].rearrange("p a j c -> p (a j c)")
        GW = J * UNITS
        stage = [xb_flat[:, s * GW:(s + 1) * GW].rearrange("p (t o) -> p t o", o=UNITS) for s in range(3)]
        stage.append(zf_flat[:, 0:GW].rearrange("p (t o) -> p t o", o=UNITS))

        w1t = xb_flat[0:KTOP, 0:4 * 512].rearrange("p (k n) -> p k n", k=4)
        w2t = xb_flat[:, 2048:3072].rearrange("p (k n) -> p k n", k=4)
        w3t = xb_flat[:, 3072:3074]
        b1t = xb_flat[:, 3074:3078]
        b2t = xb_flat[:, 3078:3080]
        ht = xb_flat[0:KTOP, 3080:5128].rearrange("p (k n) -> p k n", k=4)
        h2 = xb_flat[:, 3080:4104].rearrange("p (k n) -> p k n", k=2)
        h1 = zf_flat[:, 0:2048].rearrange("p (k n) -> p k n", k=4)
        y_row = xb_flat[0:1, 5200:5712]

        const_loaded = sem("const_loaded")
        ids_loaded = sem("ids_loaded")
        ids_next = sem("ids_next")
        stage_loaded = [sem(f"stage_loaded{s}") for s in range(4)]
        w_added = sem("w_added")
        w_high = sem("w_high")
        w_low = sem("w_low")
        identb_ready = sem("identb_ready")
        filled = sem("filled")
        pooled_zero = sem("pooled_zero")
        gathered = sem("gathered")
        split_step = sem("split_step")
        parts_stored = sem("parts_stored")
        px_loaded = [sem(f"px_loaded{s}") for s in range(2)]
        xt_stored = sem("xt_stored")
        xb_loaded = [sem(f"xb_loaded{s}") for s in range(2)]
        sel_done = sem("sel_done")
        sel_copied = sem("sel_copied")
        bt_half = sem("bt_half")
        hidden_done = sem("hidden_done")
        hidden_copied = sem("hidden_copied")
        hidden_stored = sem("hidden_stored")
        hr_loaded = {(k, p): sem(f"hr_loaded_{k}{p}") for k in "AC" for p in range(2)}
        z_done = sem("z_done")
        zh_done = sem("zh_done")
        low_pool = sem("low_pool")
        low_dve = sem("low_dve")
        pe_used = sem("pe_used")
        lo_copied = {k: sem(f"lo_copied_{k}") for k in "ABC"}
        sum_done = {k: sem(f"sum_done_{k}") for k in "ABC"}
        pooled_step = sem("pooled_step")
        pooled_done = {k: sem(f"pooled_done_{k}") for k in "ABC"}
        top_loaded = sem("top_loaded")
        top_t = sem("top_t")
        top_copied = sem("top_copied")
        top_mm = sem("top_mm")
        top_act = sem("top_act")
        out_stored = sem("out_stored")

        LOADS = 16 * MG
        ended = {"A": lambda i: i + 1, "B": lambda i: i + 2, "C": lambda i: i}

        def phase_set(kind, i):
            return (3 * i + {"B": 1, "A": 2, "C": 3}[kind]) % 2

        def tiles_of(kind, q):
            if kind == "B":
                return [(t - TG * q, t, K0 + 1 if t == 0 else (K0LAST if t == T0 - 1 else K0),
                         K0LAST if t == T0 - 1 else K0) for t in range(TG * q, min(T0, TG * q + TG))]
            base = T0 + (J * G if kind == "C" else 0)
            rows = []
            for u in range(TG):
                j = TG * (q % 2) + u
                k = KLAST if j == J - 1 else KT
                rows.append((u, base + J * (q // 2) + j, KT + 1 if (q, j) == (0, 0) else k, k))
            return rows

        def before(kind, di, q):
            o = offset_of(kind, q) + OFFSETS * di - ZL_LAG
            k, r = kind_at(o % OFFSETS)
            return k, o // OFFSETS, r

        one_b = one[:, :].unsqueeze(2).to_broadcast([P, F, SUB_D])
        x_now = lambda s: xg[:, :, SUB_D * s:SUB_D * (s + 1)]
        parts = p3[:, :, :].rearrange("p k (e n) -> p (k e) n", e=DB)
        part_of = lambda part: parts[:, :, F * part:F * (part + 1)].rearrange("p d f -> p f d")

        def split_op(engine, c, s, k):
            n = c * SUBS + s
            if k == SPLIT_OPS:
                engine.wait_ge(split_step, n * SPLIT_OPS + SPLIT_OPS + 1)
                engine.dma_start(parts_dram[bass.ds(n * SUB_BLOCKS, SUB_BLOCKS), :, :].rearrange("k b n -> b k n"),
                               p3[:, :, :]).then_inc(parts_stored, 16)
                return
            engine.wait_ge(split_step, n * SPLIT_OPS + k + 1)
            if k == 0 and not (isinstance(n, int) and n == 0):
                engine.wait_ge(parts_stored, n * 16)
                if isinstance(n, int) and n == 1:
                    engine.wait_ge(sel_done, 1)
            if k % 2 == 0:
                engine.tensor_tensor(part_of(k // 2), x_now(s), one_b, ALU.mult).then_inc(split_step, 1)
            else:
                engine.tensor_tensor(x_now(s), x_now(s), part_of(k // 2), ALU.subtract).then_inc(split_step, 1)

        block = ctx.enter_context(nc.Block())

        @block.sync
        def _(sp):
            sp.dma_start(idx[:, :], ids[:, 0, :]).then_inc(ids_loaded, 16)
            sp.dma_start(stage[0][0:K0 + 1, 0:T0, :], w0_direct).then_inc(stage_loaded[0], 16)
            sp.dma_start(stage[1][0:K0 + 1, 0:T0, :], w0_swapped).then_inc(stage_loaded[1], 16)
            sp.dma_start(sel[0:PARTS, :, :], sel_in).then_inc(const_loaded, 16)
            sp.dma_start(ident[:, :], identity_in).then_inc(const_loaded, 16)
            for n in range(2 * G):
                s = (n + 2) % 4
                if n >= 2:
                    sp.wait_ge(w_high, max(1, n - 2))
                    sp.wait_ge(w_low, max(1, n - 2))
                src = (w1, w2)[n // G]
                g = n % G
                sp.dma_start(stage[s][0:KT + 1, 0:J, :], src[:, J * g:J * (g + 1), :]).then_inc(stage_loaded[s], 16)

            def load_parts(i, k):
                sp.dma_start(px[:, k % 2, :], parts_dram[bass.ds(i, 1), :, :].rearrange("k b n -> b (k n)")
                             ).then_inc(px_loaded[k % 2], 16)

            def repeat_x(st):
                n = st.rep + 1
                if not 0 <= n < BLOCKS:
                    return
                if n == 0:
                    sp.wait_ge(w_high, 1 + 2 * G)
                    sp.wait_ge(w_low, 1 + 2 * G)
                at = n if st.expr is None else st.expr + 1
                sp.wait_ge(sel_copied, st.count(lambda i: 2 * (i + 1) + 2))
                sp.dma_start(xt_dram[bass.ds(at, 1), :, :].rearrange("k f c -> (k f) c"), a3[0:MG * J, :]
                             ).then_inc(xt_stored, 16)
                sp.wait_ge(xt_stored, st.count(lambda i: 16 * (i + 1) + 16))
                if n >= 3:
                    sp.wait_ge(z_done, st.count(lambda i: Z["C", i - 1, QA - 1]))
                for m in range(MG):
                    src = xt_dram[bass.ds(at, 1), m:m + MG * (J - 1) + 1:MG, :].to_broadcast([NGRP, J, COLS])
                    sp.dma_start(xb[NGRP * m:NGRP * (m + 1), n % 3, :, :], src).then_inc(xb_loaded[n % 2], 16)

            def store_hidden(st, kind):
                at = st.rep + (kind == "B") if st.expr is None else st.expr + (kind == "B")
                sp.wait_ge(hidden_copied, st.count(lambda i: HIDDEN[kind, i]))
                sp.dma_start(hidden_dram[kind][bass.ds(at, 1), :, :].rearrange("k n c -> (k n) c"),
                             hidden_t[0:HALF, :]).then_inc(hidden_stored, 16)

            def load_pair(st, kind, di, p):
                i = st.rep + di
                source = {"A": "B", "C": "A"}[kind]
                db = {"A": 0, "C": -1}[kind] + di
                at = st.rep + db if st.expr is None else st.expr + db
                if p == 0:
                    sp.wait_ge(hidden_stored, st.count(lambda i: 16 * HIDDEN[source, i + di - 1]))
                k = PAIR[kind, i, p]
                if k >= HR_SLOTS:
                    wk, wi, wp = PAIR_KEYS[k - HR_SLOTS]
                    wdi = wi - st.rep
                    sp.wait_ge(z_done, st.count(lambda i: Z[wk, i + wdi, 4 * wp + 3]))
                for m in range(MG):
                    src = hidden_dram[source][bass.ds(at, 1), 2 * NGRP * p:2 * NGRP * (p + 1), :].rearrange(
                        "k (g n) c -> (k n) g c", g=2)
                    sp.dma_start(hr[NGRP * m:NGRP * (m + 1), k % HR_SLOTS, :, :], src).then_inc(hr_loaded[kind, p], 16)

            def step(st):
                if st.has("C"):
                    load_pair(st, "C", 0, 1)
                repeat_x(st)
                if st.has("B"):
                    store_hidden(st, "B")
                    load_pair(st, "A", 1, 0)
                    load_pair(st, "A", 1, 1)
                if st.has("A"):
                    store_hidden(st, "A")
                    load_pair(st, "C", 1, 0)
                b = st.rep + 4
                if 1 <= b < BLOCKS:
                    if b % SUB_BLOCKS == 0 or b == 1:
                        sp.wait_ge(parts_stored, st.count(lambda i: 4 * (i + 4) + 16) if b > 1 else 16)
                    if b >= 3:
                        sp.wait_ge(sel_done, st.count(lambda i: 6 * (i + 2) + 1))
                    load_parts(b if st.expr is None else st.expr + 4, b)

            run_steps(sp, step, 2, 12, begin=-3, end=BLOCKS - 14)

            sp.wait_ge(z_done, N_GRANULES)
            sp.wait_ge(zh_done, N_GRANULES)
            sp.wait_ge(low_pool, len(LOWP))
            sp.wait_ge(low_dve, len(LOWD))
            for dst, src in ((w1t, w_top1), (ht[HALF:KTOP, :, :], dense_t), (b1t, b_top1), (w2t, w_top2),
                             (b2t, b_top2), (w3t, w_top3)):
                sp.dma_start(dst, src).then_inc(top_loaded, 16)
            sp.wait_ge(top_act, 7)
            sp.dma_start(out.rearrange("b o -> o b"), y_row).then_inc(out_stored, 16)
            sp.wait_ge(out_stored, 16)

        @block.gpsimd
        def _(pool):
            def gather(f):
                pool.indirect_dma_start(xg[:, f, :], None, tables[f],
                                        bass.IndirectOffsetOnAxis(idx[:, f:f + 1], 0)).then_inc(gathered, 16)

            pool.memset(one[:, :], 1.0)
            pool.memset(p3[:, :, :], 1.0).then_inc(split_step, 1)
            pool.wait_ge(ids_loaded, 16)
            for f in range(F):
                gather(f)
            split_op(pool, 0, 0, SPLIT_OPS)

            def low_part(st, kind, di, q):
                z = lambda i: Z[kind, i + di, q]
                slot_of = Z[kind, st.rep + di, q] - 1
                pool.wait_ge(zh_done, st.count(z))
                if Z[kind, st.rep + di, q] > ZL_SLOTS:
                    pool.wait_ge(pe_used, st.count(lambda i: z(i) - ZL_SLOTS))
                n = len(tiles_of(kind, q))
                pool.tensor_tensor(zl[0:KT, slot_of % ZL_SLOTS, 0:n, :], zf[0:KT, slot_of % ZF_SLOTS, 0:n, :],
                                   zh[0:KT, slot_of % ZH_SLOTS, 0:n, :].bitcast(f32),
                                   ALU.subtract).then_inc(low_pool, 1)

            def split_dims(c, s, o):
                split_op(pool, c, s, SPLIT_AT.index(o))
                if o == SPLIT_AT[-1]:
                    split_op(pool, c, s, SPLIT_OPS)

            def fetch(c, k, o):
                if k == 0 and o == 0:
                    pool.wait_ge(gathered, c * (16 * F))
                    pool.wait_ge(split_step, c * (SUBS * SPLIT_OPS) + 1)
                    pool.dma_start(idx[:, :], ids[:, bass.ds(c, 1), :].rearrange("p c f -> p (c f)")
                                   ).then_inc(ids_next, 16)
                if k < SPLIT_STEP:
                    f = k * len(GATHER_AT) + GATHER_AT.index(o) if o in GATHER_AT else F
                    if f < F:
                        gather(f)
                elif k < SPLIT_STEP + SUBS and o in SPLIT_AT:
                    if k == SPLIT_STEP and o == SPLIT_AT[0]:
                        pool.wait_ge(gathered, c * (16 * F) + 16 * F)
                    split_dims(c, k - SPLIT_STEP, o)

            def step(st, c=None, k=None):
                for o in range(OFFSETS):
                    kind, q = kind_at(o)
                    lk, ldi, lq = before(kind, 0, q)
                    if k == 0 and o == GATHER_AT[0]:
                        pool.wait_ge(ids_next, c * 16)
                    if st.has(lk, ldi) and (lk, st.rep + ldi, lq) in POOL_SET:
                        low_part(st, lk, ldi, lq)
                    if c is not None:
                        fetch(c, k, o)
                    elif -1 <= st.rep < SUBS - 2 and o in SPLIT_AT:
                        split_dims(0, st.rep + 2, o)

            first, per_chunk = 2, BLOCKS // CHUNKS
            for i in range(-2, first):
                step(Step(i))
            with pool.Fori(0, CHUNKS - 1) as turn:
                for k in range(per_chunk):
                    step(Step(first + k, turn * per_chunk + (first + k)), turn + 1, k)
            run_steps(pool, step, first + per_chunk * (CHUNKS - 1), 2, begin=first + per_chunk * (CHUNKS - 1))
            pool.wait_ge(parts_stored, 16 * CHUNKS * SUBS)

        @block.scalar
        def _(act):
            act.wait_ge(const_loaded, 32)
            act.activation(identb[:, :], ident[:, :], ACT.Copy).then_inc(identb_ready, 1)

            act.wait_ge(w_added, 1)
            act.activation(weights[0:K0 + 1, 0:T0, 0:UNITS], stage[0][0:K0 + 1, 0:T0, :], ACT.Copy).then_inc(w_high, 1)
            for n in range(2 * G):
                s = (n + 2) % 4
                act.wait_ge(stage_loaded[s], 16 * (1 + (n + 2) // 4))
                act.activation(weights[0:KT + 1, T0 + J * n:T0 + J * (n + 1), 0:UNITS], stage[s][0:KT + 1, :, :],
                               ACT.Copy).then_inc(w_high, 1)
            act.wait_ge(w_low, 1 + 2 * G)
            act.wait_ge(filled, 1)

            def high_part(st, kind, q):
                z = lambda i: Z[kind, i, q]
                n0 = Z[kind, st.rep, q]
                act.wait_ge(z_done, st.count(z))
                if n0 > ZH_SLOTS:
                    act.wait_ge(pe_used, st.count(lambda i: z(i) - ZH_SLOTS))
                n = len(tiles_of(kind, q))
                act.activation(zh[0:KT, (n0 - 1) % ZH_SLOTS, 0:n, :], zf[0:KT, (n0 - 1) % ZF_SLOTS, 0:n, :],
                               ACT.Copy).then_inc(zh_done, 1)

            def copy_small(st, kind, di):
                if not st.has(kind, di):
                    return
                i = st.rep + di
                act.wait_ge(pe_used, st.count(lambda i: Z[kind, i + di, (QB if kind == "B" else QA) - 1]))
                if kind == "A":
                    dst = sum_a[:, :, :]
                    if i >= 1:
                        act.wait_ge(pooled_done["A"], st.count(lambda i: ended["A"](i + di - 1)))
                        act.wait_ge(hidden_done, st.count(lambda i: HIDDEN["A", i + di - 1]))
                elif kind == "B":
                    dst = sum_bc[:, :, :]
                    if i >= 2:
                        act.wait_ge(pooled_done["C"], st.count(lambda i: ended["C"](i + di - 1)))
                    elif i >= 0:
                        act.wait_ge(pooled_done["B"], ended["B"](i - 1))
                        act.wait_ge(hidden_done, HIDDEN["B", i - 1])
                else:
                    dst = sum_bc[:, :, :]
                    act.wait_ge(pooled_done["B"], st.count(lambda i: ended["B"](i + di)) if exists("B", i) else BLOCKS)
                    if exists("B", i):
                        act.wait_ge(hidden_done, st.count(lambda i: HIDDEN["B", i + di]))
                act.activation(dst, acc[phase_set(kind, i)][:, :, UNITS:2 * UNITS], ACT.Copy).then_inc(lo_copied[kind], 1)

            def copy_hidden(st, kind):
                if not st.has(kind):
                    return
                act.wait_ge(hidden_done, st.count(lambda i: HIDDEN[kind, i]))
                if HIDDEN[kind, st.rep] > 1:
                    act.wait_ge(hidden_stored, st.count(lambda i: 16 * (HIDDEN[kind, i] - 1)))
                act.activation(hidden_t[0:HALF, :], hr_ps[0:HALF, "BA".index(kind), 0:COLS], ACT.Relu
                               ).then_inc(hidden_copied, 1)

            def copy_parts(st, di):
                if st.has("B", di):
                    act.wait_ge(sel_done, st.count(lambda i: 6 * (i + di + 1) + 1))
                    act.activation(xt3[0:PARTS, :], sel_ps[0:PARTS, 0, 0:COLS // 2].bitcast(bf16),
                                   ACT.Copy).then_inc(sel_copied, 1)

            def copy_a3(st, di):
                if st.has("B", di):
                    act.wait_ge(sel_done, st.count(lambda i: 6 * (i + di + 1) + 2))
                    if st.rep + di >= 0:
                        act.wait_ge(xt_stored, st.count(lambda i: 16 * (i + di + 1)))
                        act.wait_ge(z_done, st.count(lambda i: Z["B", i + di - 1, QB - 1]))
                    act.activation(a3[0:KT, :], sel_ps[0:KT, 1, 0:COLS], ACT.Copy).then_inc(sel_copied, 1)

            def step(st):
                for o in range(OFFSETS):
                    if o == COPY_SMALL_AT["C"] + C_LATER.get(st.rep, 0):
                        copy_small(st, "C", -1)
                    if o == COPY_SMALL_AT["A"]:
                        copy_small(st, "A", 0)
                    if o == COPY_SMALL_AT["B"]:
                        copy_small(st, "B", 0)
                    if o == XT_COPY_AT % OFFSETS:
                        copy_parts(st, 1 - XT_COPY_AT // OFFSETS)
                    if o == A3_COPY_AT % OFFSETS:
                        copy_a3(st, 1 - A3_COPY_AT // OFFSETS)
                    for kind in "BA":
                        if o == HIDDEN_COPY_AT[kind]:
                            copy_hidden(st, kind)
                    kind, q = kind_at(o)
                    if st.has(kind):
                        high_part(st, kind, q)

            run_steps(act, step, 2, 6)

            for k in range(4):
                act.wait_ge(top_t, k + 1)
                if k == 0:
                    act.wait_ge(z_done, N_GRANULES)
                src = (hr_ps, sel_ps)[k // 2][0:HALF, k % 2, :]
                act.activation(ht[0:HALF, k, :], src, ACT.Copy).then_inc(top_copied, 1)
            act.wait_ge(top_loaded, 6 * 16)
            act.wait_ge(low_pool, len(LOWP))
            act.wait_ge(low_dve, len(LOWD))
            for m in range(4):
                act.wait_ge(top_mm, m + 1)
                act.activation(h1[:, m, :], acc[m // 2][:, m % 2, :], ACT.Relu, bias=b1t[:, m:m + 1]).then_inc(top_act, 1)
            for m in range(2):
                act.wait_ge(top_mm, 5 + m)
                act.activation(h2[:, m, :], hr_ps[:, m, :], ACT.Relu, bias=b2t[:, m:m + 1]).then_inc(top_act, 1)
            act.wait_ge(top_mm, 7)
            act.activation(y_row, sel_ps[0:1, 0, :], ACT.Copy).then_inc(top_act, 1)

        @block.vector
        def _(dve):
            dve.memset(zh[:, :, :, :].bitcast(f32), 1.0).then_inc(filled, 1)
            dve.memset(pooled[:, :, :], 0.0).then_inc(pooled_zero, 1)
            dve.wait_ge(stage_loaded[0], 16)
            dve.wait_ge(stage_loaded[1], 16)
            s0, s1 = stage[0][0:K0 + 1, 0:T0, :], stage[1][0:K0 + 1, 0:T0, :]
            dve.tensor_tensor(s0, s0, s1, ALU.add).then_inc(w_added, 1)
            dve.wait_ge(w_high, 1)
            dve.tensor_tensor(weights[0:K0 + 1, 0:T0, UNITS:2 * UNITS], s0,
                              weights[0:K0 + 1, 0:T0, 0:UNITS].bitcast(f32), ALU.subtract).then_inc(w_low, 1)
            for n in range(2 * G):
                w = weights[0:KT + 1, T0 + J * n:T0 + J * (n + 1), :]
                dve.wait_ge(w_high, n + 2)
                dve.tensor_tensor(w[:, :, UNITS:2 * UNITS], stage[(n + 2) % 4][0:KT + 1, :, :],
                                  w[:, :, 0:UNITS].bitcast(f32), ALU.subtract).then_inc(w_low, 1)
            dve.wait_ge(gathered, 16 * F)
            for k in range(SPLIT_OPS):
                split_op(dve, 0, 0, k)
            dve.wait_ge(pooled_zero, 1)

            def product(st, kind, q):
                z = lambda i: Z[kind, i, q]
                n0 = Z[kind, st.rep, q]
                slot = (n0 - 1) % ZF_SLOTS
                if n0 > ZF_SLOTS:
                    was = [key for key, value in Z.items() if value == n0 - ZF_SLOTS][0]
                    wk, wi, wq = was
                    di = wi - st.rep
                    if was in POOL_SET:
                        dve.wait_ge(low_pool, st.count(lambda i: LOWP[wk, i + di, wq]))
                    else:
                        dve.wait_ge(low_dve, st.count(lambda i: LOWD[wk, i + di, wq]))
                if kind == "B":
                    for h in range(2):
                        fill = 2 * q + h
                        n = min(2, T0 - 2 * fill)
                        dve.wait_ge(sel_done, st.count(lambda i: 6 * (i + 1) + 3 + fill))
                        if fill == 0:
                            dve.wait_ge(sel_copied, st.count(lambda i: 2 * (i + 1) + 2))
                        ins = dve.tensor_tensor(
                            zf[0:KT, slot, 2 * h:2 * h + n, :],
                            a3[0:KT, :].unsqueeze(1).to_broadcast([KT, n, COLS]),
                            sel_ps[0:KT, fill % 2, 0:n * COLS].rearrange("p (t c) -> p t c", t=n), ALU.mult)
                        ins.then_inc((bt_half, z_done)[h], 1)
                    return
                b = st.rep if kind == "A" else st.rep - 1
                if q == 0 and kind == "A":
                    dve.wait_ge(xb_loaded[b % 2], st.count(lambda i: LOADS * (i // 2 + 1)))
                if q % 4 == 0:
                    dve.wait_ge(hr_loaded[kind, q // 4], st.count(lambda i: LOADS * ended[kind](i)))
                j0 = TG * (q % 2)
                dve.tensor_tensor(zf[0:KT, slot, :, :], xb[0:KT, b % 3, j0:j0 + TG, :],
                                  hr[0:KT, PAIR[kind, st.rep, q // 4] % HR_SLOTS, q // 2 % 2, :].unsqueeze(1).to_broadcast([KT, TG, COLS]),
                                  ALU.mult).then_inc(z_done, 1)

            def low_part(st, kind, di, q):
                z = lambda i: Z[kind, i + di, q]
                n0 = Z[kind, st.rep + di, q]
                dve.wait_ge(zh_done, st.count(z))
                if n0 > ZL_SLOTS:
                    dve.wait_ge(pe_used, st.count(lambda i: z(i) - ZL_SLOTS))
                n = len(tiles_of(kind, q))
                dve.tensor_tensor(zl[0:KT, (n0 - 1) % ZL_SLOTS, 0:n, :], zf[0:KT, (n0 - 1) % ZF_SLOTS, 0:n, :],
                                  zh[0:KT, (n0 - 1) % ZH_SLOTS, 0:n, :].bitcast(f32),
                                  ALU.subtract).then_inc(low_dve, 1)

            def add_and_pool(st, kind, di):
                if not st.has(kind, di):
                    return
                i = st.rep + di
                dst = sum_a[:, :, :] if kind == "A" else sum_bc[:, :, :]
                dve.wait_ge(lo_copied[kind], st.count(lambda i: ended[kind](i + di)))
                dve.tensor_tensor(dst, acc[phase_set(kind, i)][:, :, 0:UNITS], dst, ALU.add).then_inc(sum_done[kind], 1)
                first = 0 if kind == "C" else HALF
                units = UNITS - first
                at = {"B": 0, "A": HALF, "C": 2 * HALF}[kind]
                db = {"A": 0, "B": 1, "C": -1}[kind] + di
                if st.expr is None:
                    c = (st.rep + db) // (BLOCKS // CHUNKS)
                    total = pooled[:, c, at:at + units]
                else:
                    c = (st.expr + db) // (BLOCKS // CHUNKS)
                    total = pooled[:, bass.ds(c, 1), at:at + units].rearrange("p c n -> p (c n)")
                dve.wait_ge(sum_done[kind], st.count(lambda i: ended[kind](i + di)))
                dve.scalar_tensor_tensor(total, dst[:, 0, first:UNITS], 0.0, total, ALU.max, ALU.add
                                         ).then_inc(pooled_step, 1)
                dve.wait_ge(pooled_step, st.count(lambda i: steps_before(i + di, kind) + 1))
                dve.scalar_tensor_tensor(total, dst[:, 1, first:UNITS], 0.0, total, ALU.max, ALU.add
                                         ).then_inc(pooled_done[kind], 1)

            def steps_before(i, kind):
                order = []
                for s in range(-1, BLOCKS + 2):
                    for k, di, o in (("C", -1, SUM_AT["C"]), ("B", 0, SUM_AT["B"]), ("A", 0, SUM_AT["A"])):
                        if exists(k, s + di):
                            order.append((k, s + di))
                return order.index((kind, i))

            def step(st):
                for o in range(OFFSETS):
                    kind, q = kind_at(o)
                    lk, ldi, lq = before(kind, 0, q)
                    if st.has(lk, ldi) and (lk, st.rep + ldi, lq) not in POOL_SET:
                        low_part(st, lk, ldi, lq)
                    if o == SUM_AT["C"] + C_LATER.get(st.rep, 0):
                        add_and_pool(st, "C", -1)
                    if o == SUM_AT["B"]:
                        add_and_pool(st, "B", 0)
                    if o == SUM_AT["A"]:
                        add_and_pool(st, "A", 0)
                    if st.has(kind):
                        product(st, kind, q)

            run_steps(dve, step, 2, 6)

        @block.tensor
        def _(pe):
            pe.wait_ge(identb_ready, 1)
            pe.wait_ge(w_low, 1 + 2 * G)

            def transpose_hidden(st, kind):
                if not st.has(kind):
                    return
                pe.wait_ge(sum_done[kind], st.count(ended[kind]))
                if st.rep + (kind == "B") > 0:
                    pe.wait_ge(hidden_copied, st.count(lambda i: HIDDEN[kind, i - 1]))
                src = sum_a if kind == "A" else sum_bc
                for e in range(DB):
                    last = pe.matmul(hr_ps[0:HALF, "BA".index(kind), e * P:(e + 1) * P], src[:, e, 0:HALF], ident[:, :],
                                     start=True, stop=True, is_transpose=True)
                last.then_inc(hidden_done, 1)

            def select(bank, half, which):
                return pe.matmul(sel_ps[0:KT, bank, half * COLS:(half + 1) * COLS], sel[0:PARTS, which, :],
                                 xt3[0:PARTS, :], start=True, stop=True)

            def tensor_fill(st, what, di):
                if not st.has("B", di):
                    return
                b = st.rep + di + 1
                if what == "T":
                    if b == 0:
                        pe.wait_ge(split_step, SPLIT_OPS + 1)
                    else:
                        pe.wait_ge(px_loaded[b % 2], st.count(lambda i: 16 * ((i + di + 2) // 2)))
                    if b >= 1:
                        pe.wait_ge(bt_half, st.count(lambda i: 2 * (i + di) + 2))
                    source = p3[:, 0, :] if b == 0 else px[:, b % 2, :]
                    for e in range(DB):
                        last = pe.transpose(sel_ps[0:PARTS, 0, e * P // 2:(e + 1) * P // 2].bitcast(bf16),
                                            source[:, e * PARTS:(e + 1) * PARTS], identb[:, :])
                    last.then_inc(sel_done, 1)
                    return
                if what == "A3":
                    pe.wait_ge(sel_copied, st.count(lambda i: 2 * (i + di + 1) + 1))
                    if b >= 1:
                        pe.wait_ge(z_done, st.count(lambda i: Z["B", i + di - 1, 1]))
                    select(1, 0, 0).then_inc(sel_done, 1)
                    return
                if what == 1:
                    pe.wait_ge(sel_copied, st.count(lambda i: 2 * (i + di + 1) + 2))
                if what == 2:
                    pe.wait_ge(bt_half, st.count(lambda i: 2 * (i + di + 1) + 1))
                if what == 3:
                    pe.wait_ge(z_done, st.count(lambda i: Z["B", i + di, 0]))
                for h in range(min(2, T0 - 2 * what)):
                    last = select(what % 2, h, 1 + 2 * what + h)
                last.then_inc(sel_done, 1)

            def granule(st, kind, q):
                i = st.rep
                if q == 0:
                    if kind == "B" and i >= 1:
                        pe.wait_ge(sum_done["A"], st.count(lambda i: ended["A"](i - 1)))
                    elif kind == "A" and i >= 2:
                        pe.wait_ge(sum_done["C"], st.count(lambda i: ended["C"](i - 1)))
                    elif kind == "A":
                        pe.wait_ge(sum_done["B"], ended["B"](i - 1))
                    elif kind == "C" and i <= BLOCKS - 2:
                        pe.wait_ge(sum_done["B"], st.count(ended["B"]))
                    elif kind == "C":
                        pe.wait_ge(sum_done["A"], i)
                z = lambda i: Z[kind, i, q]
                n0 = Z[kind, i, q] - 1
                key = (kind, i, q)
                pe.wait_ge(zh_done, st.count(z))
                if key in POOL_SET:
                    pe.wait_ge(low_pool, st.count(lambda i: LOWP[kind, i, q]))
                else:
                    pe.wait_ge(low_dve, st.count(lambda i: LOWD[kind, i, q]))
                phase = acc[phase_set(kind, i)]
                last_q = q == (QB if kind == "B" else QA) - 1
                tiles = tiles_of(kind, q)
                for e in range(DB):
                    for u, w, k_high, k_low in tiles:
                        high = zh[0:k_high, n0 % ZH_SLOTS, u, e * P:(e + 1) * P]
                        low = zl[0:k_low, n0 % ZL_SLOTS, u, e * P:(e + 1) * P]
                        pe.matmul(phase[:, e, 0:2 * UNITS], high, weights[0:k_high, w, :],
                                  start=(q == 0 and u == 0), stop=False)
                        last = pe.matmul(phase[:, e, UNITS:2 * UNITS], low, weights[0:k_low, w, 0:UNITS],
                                         start=False, stop=(last_q and u == len(tiles) - 1))
                last.then_inc(pe_used, 1)

            def step(st):
                for o in range(OFFSETS):
                    for kind in "BA":
                        if o == HIDDEN_AT[kind]:
                            transpose_hidden(st, kind)
                    for at, what, di in FILLS:
                        if at == o:
                            tensor_fill(st, what, di)
                    kind, q = kind_at(o)
                    if st.has(kind):
                        granule(st, kind, q)

            run_steps(pe, step, 2, 2)

            for kind in "ABC":
                pe.wait_ge(pooled_done[kind], BLOCKS)
            for k in range(4):
                dst = (hr_ps, sel_ps)[k // 2]
                for c in range(CHUNKS):
                    last = pe.matmul(dst[0:HALF, k % 2, c * P:(c + 1) * P], pooled[:, c, k * HALF:(k + 1) * HALF],
                                     ident[:, :], start=True, stop=True, is_transpose=True)
                last.then_inc(top_t, 1)
            pe.wait_ge(top_loaded, 6 * 16)
            pe.wait_ge(top_copied, 4)
            for m in range(4):
                dst = acc[m // 2][:, m % 2, :]
                for k in range(4):
                    last = pe.matmul(dst, w1t[:, k, m * P:(m + 1) * P], ht[:, k, :], start=(k == 0), stop=(k == 3))
                last.then_inc(top_mm, 1)
            pe.wait_ge(top_act, 4)
            for m in range(2):
                for k in range(4):
                    last = pe.matmul(hr_ps[:, m, :], w2t[:, k, m * P:(m + 1) * P], h1[:, k, :], start=(k == 0),
                                     stop=(k == 3))
                last.then_inc(top_mm, 1)
            pe.wait_ge(top_act, 6)
            for k in range(2):
                last = pe.matmul(sel_ps[0:1, 0, :], w3t[:, k:k + 1], h2[:, k, :], start=(k == 0), stop=(k == 1))
            last.then_inc(top_mm, 1)


def selection():
    import numpy as np
    s = np.zeros((PARTS, 1 + T0, KT), np.float32)
    for part in range(3):
        for p in range(K0):
            s[F * part + p % F, 0, p] = 1
            for t in range(T0):
                shift = SPT * t + p // F
                if shift < SHIFTS:
                    s[F * part + (p % F + shift) % F, 1 + t, p] = 1
    s[PARTS - 1, 0:2, K0] = 1
    return s


def kernel(**inputs):
    import ml_dtypes
    import numpy as np
    import concourse.bacc as bacc
    from concourse import mybir
    from concourse.bass_utils import run_bass_kernel_spmd

    a = {k: np.ascontiguousarray(v) for k, v in inputs.items()}

    zero = np.zeros((1, UNITS), np.float32)
    rows0 = np.concatenate([a["L0_rec_W0"], a["L0_rec_b0"][None], zero])
    bias_row, zero_row = F * F, F * F + 1
    direct = np.full((K0 + 1, T0), zero_row)
    swapped = np.full((K0 + 1, T0), zero_row)
    for t in range(T0):
        for p in range(K0):
            s, m = SPT * t + p // F, p % F
            if s < SHIFTS:
                n = (m + s) % F
                direct[p, t] = m * F + n
                if s:
                    swapped[p, t] = n * F + m
    direct[K0, 0] = bias_row

    tiles = np.full((KT + 1, G * J), F * HALF + 1)
    for g in range(G):
        for j in range(J):
            for p in range(KT):
                m, n = MG * j + p // NGRP, NGRP * g + p % NGRP
                if m < F:
                    tiles[p, J * g + j] = m * HALF + n
    tiles[KT, 0] = F * HALF

    def packed(layer):
        rows = np.concatenate([a[f"L0_rec_W{layer}"], a[f"L0_rec_b{layer}"][None], zero])
        return rows[tiles]

    arrays = {
        "ids": np.ascontiguousarray(a["ids"].reshape(CHUNKS, P, F).transpose(1, 0, 2)),
        "w0_direct": rows0[direct], "w0_swapped": rows0[swapped],
        "w1": packed(1), "w2": packed(2),
        "sel": selection().astype(ml_dtypes.bfloat16),
        "identity": np.eye(P, dtype=np.float32),
        "w_top1": np.ascontiguousarray(np.concatenate(
            [a["W_top1"][:4 * HALF].reshape(4, HALF, 512), a["W_top1"][4 * HALF:].reshape(4, DENSE // 4, 512)],
            axis=1).transpose(1, 0, 2)),
        "b_top1": np.ascontiguousarray(a["b_top1"].reshape(4, P).T),
        "w_top2": np.ascontiguousarray(a["W_top2"].reshape(4, P, 256).transpose(1, 0, 2)),
        "b_top2": np.ascontiguousarray(a["b_top2"].reshape(2, P).T),
        "w_top3": np.ascontiguousarray(a["W_top3"].reshape(2, P).T),
        "dense_t": np.ascontiguousarray(a["dense_ctx"].T.reshape(4, DENSE // 4, B).transpose(1, 0, 2)),
    }
    for f in range(F):
        arrays[f"tbl_{f}"] = a[f"tbl_{f}"]

    nc = bacc.Bacc("TRN2", target_bir_lowering=False, num_devices=1)
    dram = {name: nc.dram_tensor(name, v.shape, mybir.dt.from_np(v.dtype), kind="ExternalInput").ap()
            for name, v in arrays.items()}
    out = nc.dram_tensor("y", (B, 1), mybir.dt.float32, kind="ExternalOutput").ap()
    build(nc, dram["ids"], [dram[f"tbl_{f}"] for f in range(F)], dram["w0_direct"], dram["w0_swapped"], dram["w1"],
          dram["w2"], dram["sel"], dram["identity"], dram["w_top1"], dram["b_top1"],
          dram["w_top2"], dram["b_top2"], dram["w_top3"], dram["dense_t"], out)
    result = run_bass_kernel_spmd(nc, [arrays], core_ids=[0])
    return result.results[0]["y"]
```
